# Optimizing a Trainium2 kernel written in Bass

```python
import numpy as np
import jax
import jax.numpy as jnp

def _softmax(x, axis=-1):
    return jax.nn.softmax(x, axis=axis)
def _gelu(x):
    return jax.nn.gelu(x, approximate=True)
def _silu(x):
    return jax.nn.silu(x)
def _sigmoid(x):
    return jax.nn.sigmoid(x)
def _layernorm(x, axis=-1, eps=1e-5):
    m = jnp.mean(x, axis=axis, keepdims=True)
    v = jnp.var(x, axis=axis, keepdims=True)
    return (x - m) / jnp.sqrt(v + eps)
def _scatter_add(tgt, idx, src, axis=0):
    return tgt.at[idx].add(src)
def _segment_sum(src, seg, n):
    return jax.ops.segment_sum(src, seg, n)

kernel_name = 'mk_conv_seq_d1_conv_nchw256_29d320'

def setup_inputs(seed: int = 0):
    np.random.seed(seed)
    _w = jnp.asarray
    def _rec_inputs():
        import jax
        import jax.numpy as jnp
        _gk = jax.random.key(seed)
        x = -0.0003972 + 0.9999 * jax.random.normal(jax.random.fold_in(_gk, 1), (8, 256, 80, 80), jnp.float32)
        return x
    x = _rec_inputs()
    def _L0_conv_setup():
        import jax, jax.numpy as jnp
        import numpy as np
        BN_EPS = 1e-05

        def conv1x1(x, w, b):
            return jnp.einsum('bchw,oc->bohw', x, w) + b[None, :, None, None]

        def dwconv3(x, w, b):
            y = jax.lax.conv_general_dilated(x, w, window_strides=(1, 1), padding='SAME', feature_group_count=x.shape[1], dimension_numbers=('NCHW', 'OIHW', 'NCHW'))
            return y + b[None, :, None, None]
        key = jax.random.key(seed)
        B, C, H, W, E = (8, 256, 80, 80, 2)
        ks = jax.random.split(key, 16)

        def n(k, shape, sc=0.02):
            return jax.random.normal(k, shape, dtype=jnp.float32) * sc
        return {'x': jax.random.normal(ks[0], (B, C, H, W), dtype=jnp.float32), 'bn_gamma': jnp.ones((C,), jnp.float32), 'bn_beta': jnp.zeros((C,), jnp.float32), 'bn_mean': n(ks[1], (C,), 0.1), 'bn_var': jnp.abs(n(ks[2], (C,), 0.5)) + 1.0, 'alpha_real': n(ks[3], (1, C, 1, 1), 0.1), 'alpha_imag': n(ks[4], (1, C, 1, 1), 0.1), 'pi_w': n(ks[5], (C, C)), 'pi_b': jnp.zeros((C,), jnp.float32), 'dw_w': n(ks[6], (C, 1, 3, 3)), 'dw_b': jnp.zeros((C,), jnp.float32), 'fpw_w': n(ks[7], (C, C)), 'fpw_b': jnp.zeros((C,), jnp.float32), 'ffn1_w': n(ks[8], (C * E, C)), 'ffn1_b': jnp.zeros((C * E,), jnp.float32), 'ffn2_w': n(ks[9], (C, C * E)), 'ffn2_b': jnp.zeros((C,), jnp.float32), 'po_w': n(ks[10], (C, C)), 'po_b': jnp.zeros((C,), jnp.float32), 'post_w': n(ks[11], (C, C)), 'post_b': jnp.zeros((C,), jnp.float32)}
    _L0_conv_all = _L0_conv_setup()
    _L0_conv_in = {k: v for k, v in _L0_conv_all.items() if k in ('bn_gamma', 'bn_beta', 'bn_mean', 'bn_var', 'alpha_real', 'alpha_imag', 'pi_w', 'pi_b', 'dw_w', 'dw_b', 'fpw_w', 'fpw_b', 'ffn1_w', 'ffn1_b', 'ffn2_w', 'ffn2_b', 'po_w', 'po_b', 'post_w', 'post_b', )}
    del _L0_conv_all

    return {
        "x": x,
        "L0_conv_bn_gamma": _L0_conv_in["bn_gamma"],
        "L0_conv_bn_beta": _L0_conv_in["bn_beta"],
        "L0_conv_bn_mean": _L0_conv_in["bn_mean"],
        "L0_conv_bn_var": _L0_conv_in["bn_var"],
        "L0_conv_alpha_real": _L0_conv_in["alpha_real"],
        "L0_conv_alpha_imag": _L0_conv_in["alpha_imag"],
        "L0_conv_pi_w": _L0_conv_in["pi_w"],
        "L0_conv_pi_b": _L0_conv_in["pi_b"],
        "L0_conv_dw_w": _L0_conv_in["dw_w"],
        "L0_conv_dw_b": _L0_conv_in["dw_b"],
        "L0_conv_fpw_w": _L0_conv_in["fpw_w"],
        "L0_conv_fpw_b": _L0_conv_in["fpw_b"],
        "L0_conv_ffn1_w": _L0_conv_in["ffn1_w"],
        "L0_conv_ffn1_b": _L0_conv_in["ffn1_b"],
        "L0_conv_ffn2_w": _L0_conv_in["ffn2_w"],
        "L0_conv_ffn2_b": _L0_conv_in["ffn2_b"],
        "L0_conv_po_w": _L0_conv_in["po_w"],
        "L0_conv_po_b": _L0_conv_in["po_b"],
        "L0_conv_post_w": _L0_conv_in["post_w"],
        "L0_conv_post_b": _L0_conv_in["post_b"],
    }

def reference(x, L0_conv_bn_gamma, L0_conv_bn_beta, L0_conv_bn_mean, L0_conv_bn_var, L0_conv_alpha_real, L0_conv_alpha_imag, L0_conv_pi_w, L0_conv_pi_b, L0_conv_dw_w, L0_conv_dw_b, L0_conv_fpw_w, L0_conv_fpw_b, L0_conv_ffn1_w, L0_conv_ffn1_b, L0_conv_ffn2_w, L0_conv_ffn2_b, L0_conv_po_w, L0_conv_po_b, L0_conv_post_w, L0_conv_post_b):
    import jax
    import jax.numpy as jnp
    def _L0_conv_ref(x, bn_gamma, bn_beta, bn_mean, bn_var, alpha_real, alpha_imag, pi_w, pi_b, dw_w, dw_b, fpw_w, fpw_b, ffn1_w, ffn1_b, ffn2_w, ffn2_b, po_w, po_b, post_w, post_b):
        import jax, jax.numpy as jnp
        import numpy as np
        BN_EPS = 1e-05

        def conv1x1(x, w, b):
            return jnp.einsum('bchw,oc->bohw', x, w) + b[None, :, None, None]

        def dwconv3(x, w, b):
            y = jax.lax.conv_general_dilated(x, w, window_strides=(1, 1), padding='SAME', feature_group_count=x.shape[1], dimension_numbers=('NCHW', 'OIHW', 'NCHW'))
            return y + b[None, :, None, None]
        res = x
        inv = jax.lax.rsqrt(bn_var + BN_EPS)
        h = (x - bn_mean[None, :, None, None]) * (bn_gamma * inv)[None, :, None, None] + bn_beta[None, :, None, None]
        H, W = (h.shape[2], h.shape[3])
        X = jnp.fft.rfft2(h, norm='ortho')
        Y = X * (alpha_real + 1j * alpha_imag)
        h = jnp.fft.irfft2(Y, s=(H, W), norm='ortho')
        res2 = h
        t = conv1x1(h, pi_w, pi_b)
        y = jax.nn.gelu(dwconv3(t, dw_w, dw_b), approximate=False)
        y = conv1x1(y, fpw_w, fpw_b)
        y = jax.nn.gelu(conv1x1(y, ffn1_w, ffn1_b), approximate=False)
        y = conv1x1(y, ffn2_w, ffn2_b)
        h = conv1x1(y, po_w, po_b) + res2
        out = conv1x1(h, post_w, post_b)
        return out + res

    def _gn(v, G=32, eps=1e-5):
        B_, C_, H_, W_ = v.shape
        g = v.reshape(B_, G, C_ // G, H_, W_)
        m = jnp.mean(g, axis=(2, 3, 4), keepdims=True)
        s = jnp.var(g, axis=(2, 3, 4), keepdims=True)
        return ((g - m) / jnp.sqrt(s + eps)).reshape(v.shape)

    def _ln_c(v, eps=1e-6):
        m = jnp.mean(v, axis=1, keepdims=True)
        s = jnp.var(v, axis=1, keepdims=True)
        return (v - m) / jnp.sqrt(s + eps)

    def _ln_t(v, eps=1e-5):
        m = jnp.mean(v, axis=-1, keepdims=True)
        s = jnp.var(v, axis=-1, keepdims=True)
        return (v - m) / jnp.sqrt(s + eps)

    def _to_tokens(v):
        B_, C_, H_, W_ = v.shape
        return v.reshape(B_, C_, H_ * W_).transpose(0, 2, 1)
    def _from_tokens(t, like):
        B_, C_, H_, W_ = like.shape
        return t.transpose(0, 2, 1).reshape(B_, C_, H_, W_)

    x = _L0_conv_ref(x, L0_conv_bn_gamma, L0_conv_bn_beta, L0_conv_bn_mean, L0_conv_bn_var, L0_conv_alpha_real, L0_conv_alpha_imag, L0_conv_pi_w, L0_conv_pi_b, L0_conv_dw_w, L0_conv_dw_b, L0_conv_fpw_w, L0_conv_fpw_b, L0_conv_ffn1_w, L0_conv_ffn1_b, L0_conv_ffn2_w, L0_conv_ffn2_b, L0_conv_po_w, L0_conv_po_b, L0_conv_post_w, L0_conv_post_b)
    return x


_drawn_inputs = setup_inputs


def setup_inputs(seed=0):
    import zlib

    import numpy as np

    out = dict(_drawn_inputs(seed))
    spreads = {'L0_conv_bn_gamma': (1.0, 0.6),
     'L0_conv_bn_beta': (0.0, 0.8),
     'L0_conv_pi_b': (0.0, 0.8),
     'L0_conv_dw_b': (0.0, 0.8),
     'L0_conv_fpw_b': (0.0, 0.8),
     'L0_conv_ffn1_b': (0.0, 0.8),
     'L0_conv_ffn2_b': (0.0, 0.8),
     'L0_conv_po_b': (0.0, 0.8),
     'L0_conv_post_b': (0.0, 0.516)}
    factors = {'L0_conv_bn_mean': 49.236,
     'L0_conv_bn_var': 200.0,
     'L0_conv_pi_w': 8.0,
     'L0_conv_dw_w': 8.0,
     'L0_conv_fpw_w': 8.0,
     'L0_conv_ffn1_w': 8.0,
     'L0_conv_ffn2_w': 8.0,
     'L0_conv_po_w': 5.77,
     'L0_conv_alpha_imag': 3.187}
    for name, (base, spread) in spreads.items():
        noise = np.random.default_rng([zlib.crc32(name.encode()), seed]).standard_normal(out[name].shape)
        drawn = base * np.exp(spread * noise) if base else spread * noise
        out[name] = jnp.asarray(drawn.astype(out[name].dtype))
    for name, factor in factors.items():
        out[name] = (out[name] * factor).astype(out[name].dtype)
    return out
```

```python
import concourse.bass as bass
from concourse import mybir
from contextlib import ExitStack

B, C, H, W = 8, 256, 80, 80
E2 = 2 * C
KC = C // 128
KE = E2 // 128
ROWS = 10
HALF = ROWS // 2
NPX = ROWS * W
NHALF = HALF * W
TPI = H // ROWS
TILES = B * TPI
LAST_LAG = 4
HW = W // 2
GROUP = 3
GROUPS = ROWS // GROUP
assert GROUPS * GROUP == ROWS - 1
Z_ROW = 86
assert all((r * Z_ROW) // 512 == (r * Z_ROW + W - 1) // 512 for r in range(ROWS))
assert all((g * GROUP * Z_ROW) // 512 == ((g * GROUP + GROUP - 1) * Z_ROW) // 512 for g in range(GROUPS))
T1_SLOTS = 4
T1_ROWS, T1_COLS = ROWS + 2, W + 2
RES_SLOTS = 4
TAPS = [(0, -1), (0, 1), (-1, -1), (-1, 0), (-1, 1), (1, -1), (1, 0), (1, 1)]
CONV_STEPS = KC * len(TAPS)
EPS = 1e-5
BN_STEPS = 2 + 2 * 4 + 6 + KC
VEC = {n: KC * i for i, n in enumerate(
    ["gamma", "beta", "mean", "var", "ar", "ai", "pi_b", "dw_b", "fpw_b", "ffn2_b", "po_b", "post_b"])}
VEC["ffn1_b"] = KC * 12
VEC["dw_w"] = VEC["ffn1_b"] + KE
NVEC = VEC["dw_w"] + 9 * KC


class Tile:

    def __init__(self, image, j):
        self.image, self.j = image, j

    def back(self, lag):
        j = self.j - lag
        return Tile(self.image + j // TPI, j % TPI) if j // TPI else Tile(self.image, j)

    @property
    def known(self):
        return isinstance(self.image, int)

    @property
    def exists(self):
        return not self.known or 0 <= self.image * TPI + self.j < TILES

    def count(self, per_tile, more=0):
        return self.image * (TPI * per_tile) + (self.j * per_tile + more)

    def slot_count(self, slots, more=0, by=16):
        return self.image * (by * TPI // slots) + by * (self.j // slots + more)


def wait_for(eng, sem, tile, per_tile, more):
    if tile.exists and (not tile.known or tile.count(per_tile, more) > 0):
        eng.wait_ge(sem, tile.count(per_tile, more))


def wait_slot(eng, sem, tile, slots, more, by=16):
    if tile.exists and (not tile.known or tile.slot_count(slots, more, by) > 0):
        eng.wait_ge(sem, tile.slot_count(slots, more, by))


def run_ticks(eng, tick):
    for j in range(TPI):
        tick(Tile(0, j))
    with eng.Fori(1, B) as image:
        for j in range(TPI):
            tick(Tile(image, j))
    for j in range(LAST_LAG):
        tick(Tile(B, j))


def conv_block_program(nc, x, xw3, xw1, vec, toep3, toep1, pi_t, fpw, ffn1_t, ffn2, po, post_t, out):
    f32 = mybir.dt.float32
    f32r = mybir.dt.float32r
    ALU = mybir.AluOpType
    ACT = mybir.ActivationFunctionType

    x_v = x.rearrange("b (k p) (j r) w -> b j p k (r w)", p=128, r=ROWS)
    out_v = out.rearrange("b (k p) (j r) w -> b j p k (r w)", p=128, r=ROWS)

    ctx = ExitStack()
    with ctx:
        def sb(name, shape, dt=f32):
            return ctx.enter_context(nc.sbuf_tensor(name, shape, dt))

        def sem(name):
            return ctx.enter_context(nc.semaphore(name))

        pi_hl = [sb(f"pi_{s}", [128, KC, C], f32r) for s in "hl"]
        post_hl = [sb(f"post_{s}", [128, KC, C], f32r) for s in "hl"]
        w1_hl = [sb(f"w1_{s}", [128, KC, E2], f32r) for s in "hl"]
        w2_hl = [sb(f"w2_{s}", [128, KE, C], f32r) for s in "hl"]
        toep3_sb = sb("toep3_sb", [GROUP * HW, 2, GROUP * HW])
        toep1_sb = sb("toep1_sb", [W, W])
        vecs = sb("vecs", [128, NVEC])
        bn = sb("bn", [128, 8, KC])
        b1 = sb("b1", [128, KE])
        b_out = sb("b_out", [128, KC])

        x_sb = sb("x_sb", [128, 2, KC, NPX])
        xw3_sb = sb("xw3_sb", [GROUP * HW, 2, GROUPS * 2, C])
        xw1_sb = sb("xw1_sb", [W, 2, C])
        xres_sb = sb("xres_sb", [128, 2, KC, NPX])
        res_h = sb("res_h", [128, RES_SLOTS, KC, NPX], f32r)
        res_l = sb("res_l", [128, RES_SLOTS, KC, NPX], f32r)
        t1_sb = sb("t1_sb", [128, T1_SLOTS, KC, T1_ROWS, T1_COLS])
        acc = sb("acc", [128, 2, KC, NPX])
        g1_h = sb("g1_h", [128, KC, NPX], f32r)
        g1_l = sb("g1_l", [128, KC, NPX], f32r)
        g2_sb = sb("g2_sb", [128, 2, NPX])
        g2_h = sb("g2_h", [128, KE, NPX], f32r)
        g2_l = sb("g2_l", [128, KE, NPX], f32r)
        area = [[ctx.enter_context(nc.psum_tensor(f"area_{p}{c}", [128, 2, 512], f32)) for c in range(2)]
                for p in range(2)]

        raw = t1_sb[:, :, :, :, :].rearrange("p s k r w -> p (s k r w)")
        at = [0]

        def raw_view(chunks, n):
            v = raw[:, at[0]:at[0] + chunks * n].rearrange("p (k n) -> p k n", k=chunks)
            at[0] += chunks * n
            return v

        r_pi, r_fpw, r_ffn1 = raw_view(KC, C), raw_view(KC, C), raw_view(KC, E2)
        r_ffn2, r_po, r_post, r_p = raw_view(KC, E2), raw_view(KC, C), raw_view(KC, C), raw_view(KC, C)

        vecs_loaded, raw_loaded, toep_loaded = sem("vecs_loaded"), sem("raw_loaded"), sem("toep_loaded")
        x_loaded = [sem(f"x_loaded{i}") for i in range(2)]
        xw_loaded = [sem(f"xw_loaded{i}") for i in range(2)]
        xres_loaded = [sem(f"xres_loaded{i}") for i in range(2)]
        out_stored = [sem(f"out_stored{i}") for i in range(2)]
        bn_step = sem("bn_step")
        root_done = sem("root_done")
        made = sem("made")
        kept = sem("kept")
        split_h = sem("split_h")
        pads_zeroed = sem("pads_zeroed")
        z_done = sem("z_done")
        resa_done = sem("resa_done")
        res2_done = sem("res2_done")
        res_h_done = sem("res_h_done")
        res_l_done = sem("res_l_done")
        t1_ready = sem("t1_ready")
        t1_taken = sem("t1_taken")
        conv_step = sem("conv_step")
        gelu1_done = sem("gelu1_done")
        g1_h_done = sem("g1_h_done")
        g1_l_done = sem("g1_l_done")
        f1_ready = sem("f1_ready")
        gelu2_done = sem("gelu2_done")
        g2_h_done = sem("g2_h_done")
        g2_l_done = sem("g2_l_done")
        out_ready = sem("out_ready")
        out_added = sem("out_added")

        def v(name, k):
            return vecs[:, VEC[name] + k:VEC[name] + k + 1]

        def vv(name):
            return vecs[:, VEC[name]:VEC[name] + KC]

        gain_x, shift_x, gain_z, centre_b = 4, 5, 6, 7

        def bn_col(row, k):
            return bn[:, row, k:k + 1]

        def tap_w(dh, dw, k):
            i = VEC["dw_w"] + 9 * k + 3 * (dh + 1) + (dw + 1)
            return vecs[:, i:i + 1]

        def banks(ap):
            return ap.rearrange("p (h n) -> p h n", h=2)

        def image_rows(ap):
            return ap.rearrange("p (r w) -> p r w", w=W)

        block = ctx.enter_context(nc.Block())

        @block.sync
        def _(sp):
            sp.dma_start(vecs[:, :], vec).then_inc(vecs_loaded, 16)
            for dst, src in ((r_po, po), (r_post, post_t), (r_ffn2, ffn2), (r_fpw, fpw), (r_ffn1, ffn1_t),
                             (r_pi, pi_t)):
                sp.dma_start(dst, src.rearrange("(k p) n -> p k n", p=128)).then_inc(raw_loaded, 16)
            sp.dma_start(toep3_sb[:, :, :], toep3).then_inc(toep_loaded, 16)
            sp.dma_start(toep1_sb[:, :], toep1).then_inc(toep_loaded, 16)

            def tick(t):
                if t.exists:
                    wait_for(sp, z_done, t.back(2), 2, 2)
                    sp.dma_start(xw3_sb[:, t.j % 2, :, :], xw3[t.image, t.j]).then_inc(xw_loaded[t.j % 2], 16)
                    sp.dma_start(xw1_sb[:, t.j % 2, :], xw1[t.image, t.j]).then_inc(xw_loaded[t.j % 2], 16)
                    wait_for(sp, res_l_done, t.back(2), 1, 1)
                    sp.dma_start(x_sb[:, t.j % 2, :, :], x_v[t.image, t.j]).then_inc(x_loaded[t.j % 2], 16)
                o = t.back(LAST_LAG)
                if o.exists:
                    wait_for(sp, out_added, o, 2, 2)
                    sp.dma_start(out_v[o.image, o.j], xres_sb[:, o.j % 2, :, :]).then_inc(out_stored[o.j % 2], 16)
                r = t.back(LAST_LAG - 2)
                if r.exists:
                    wait_slot(sp, out_stored[r.j % 2], r, 2, 0)
                    sp.dma_start(xres_sb[:, r.j % 2, :, :], x_v[r.image, r.j]).then_inc(xres_loaded[r.j % 2], 16)

            run_ticks(sp, tick)
            for s in range(2):
                sp.wait_ge(out_stored[s], 16 * TILES // 2)

        @block.tensor
        def _(pe):
            mm = nc.tensor.matmul

            def products(pairs, dst, stat, mov):
                n = len(pairs)
                for i, (ws, ms) in enumerate(pairs):
                    for p, (a, b) in enumerate(((0, 0), (1, 0), (0, 1))):
                        last = mm(dst, ws(stat[a]), ms(mov[b]), start=(i == 0 and p == 0),
                                  stop=(i == n - 1 and p == 2))
                return last

            pe.wait_ge(raw_loaded, 16 * 6)
            pe.wait_ge(vecs_loaded, 16)
            for k in range(KC):
                for q in range(KC):
                    last = mm(area[0][0][:, k, 0:C], r_po[:, q, k * 128:(k + 1) * 128], r_post[:, q, :],
                              start=(q == 0), stop=(q == KC - 1))
            last.then_inc(made, 1)
            for k in range(KC):
                for q in range(KC):
                    last = mm(area[0][1][:, k, 0:E2], r_fpw[:, q, k * 128:(k + 1) * 128], r_ffn1[:, q, :],
                              start=(q == 0), stop=(q == KC - 1))
            for o in range(KE):
                for q in range(KC):
                    last = mm(area[1][0][:, 0, 2 * o:2 * o + 1], r_ffn1[:, q, o * 128:(o + 1) * 128],
                              v("fpw_b", q), start=(q == 0), stop=(q == KC - 1))
            last.then_inc(made, 1)
            pe.wait_ge(kept, 1)
            for k in range(KE):
                for q in range(KC):
                    last = mm(area[1][1][:, k // 2, (k % 2) * C:(k % 2 + 1) * C],
                              r_ffn2[:, q, k * 128:(k + 1) * 128], r_p[:, q, :],
                              start=(q == 0), stop=(q == KC - 1))
            for o in range(KC):
                for i, (w, b) in enumerate(((r_p, "ffn2_b"), (r_post, "po_b"))):
                    for q in range(KC):
                        last = mm(area[1][0][:, 1, 2 * o:2 * o + 1], w[:, q, o * 128:(o + 1) * 128], v(b, q),
                                  start=(i == 0 and q == 0), stop=(i == 1 and q == KC - 1))
            last.then_inc(made, 1)
            pe.wait_ge(kept, 4)
            pe.wait_ge(toep_loaded, 32)

            def tick(t):
                pair_a, pair_b = area[t.j % 2], area[1 - t.j % 2]
                s = t.back(1)
                if s.exists:
                    wait_for(pe, res_h_done, s, 1, 1)
                    wait_for(pe, res_l_done, s, 1, 1)
                    for c in range(KC):
                        wait_for(pe, gelu2_done, t.back(4), 4, 3 + c)
                        for h in range(2):
                            pairs = [(lambda w, k=k: w[:, k, c * 128:(c + 1) * 128],
                                      lambda m, k=k: m[:, s.j % RES_SLOTS, k, h * NHALF:(h + 1) * NHALF])
                                     for k in range(KC)]
                            last = products(pairs, pair_a[c][:, h, 0:NHALF], pi_hl, (res_h, res_l))
                        last.then_inc(t1_ready, 1)
                if t.exists:
                    wait_for(pe, out_added, t.back(4), 2, 2)
                    wait_slot(pe, xw_loaded[t.j % 2], t, 2, 1, 32)
                    for c in range(KC):
                        z = pair_b[c][:, :, :].rearrange("p h n -> p (h n)")
                        for g in range(GROUPS):
                            for e in range(2):
                                rows = z[:, g * GROUP * Z_ROW:(g + 1) * GROUP * Z_ROW]
                                mm(rows.rearrange("p (r n) -> p r n", n=Z_ROW)[:, :, e * HW:(e + 1) * HW],
                                   xw3_sb[:, t.j % 2, 2 * g + e, c * 128:(c + 1) * 128], toep3_sb[:, e, :],
                                   start=True, stop=True)
                        mm(z[:, (ROWS - 1) * Z_ROW:(ROWS - 1) * Z_ROW + W],
                           xw1_sb[:, t.j % 2, c * 128:(c + 1) * 128], toep1_sb[:, :],
                           start=True, stop=True).then_inc(z_done, 1)
                u = t.back(3)
                if u.exists:
                    wait_for(pe, g1_h_done, u, 1, 1)
                    wait_for(pe, g1_l_done, u, 1, 1)
                    for c in range(KE):
                        dst = (pair_a, pair_b)[c // 2][c % 2]
                        if c < 2:
                            if s.exists:
                                wait_for(pe, t1_taken, s, 8, 7 + c)
                            else:
                                wait_for(pe, gelu2_done, t.back(4), 4, 3 + c)
                        else:
                            if t.exists:
                                wait_for(pe, res2_done, t, 4, 2 * (c - 1))
                            else:
                                wait_for(pe, out_added, t.back(4), 2, c - 1)
                        for h in range(2):
                            pairs = [(lambda w, k=k: w[:, k, c * 128:(c + 1) * 128],
                                      lambda m, k=k: m[:, k, h * NHALF:(h + 1) * NHALF]) for k in range(KC)]
                            last = products(pairs, dst[:, h, 0:NHALF], w1_hl, (g1_h, g1_l))
                        last.then_inc(f1_ready, 1)
                    for c in range(KC):
                        wait_for(pe, gelu2_done, u, 4, 1 + c)
                        for h in range(2):
                            for k in range(KC):
                                for p, (a, b) in enumerate(((0, 0), (1, 0), (0, 1))):
                                    mm(pair_a[c][:, h, 0:NHALF], post_hl[a][:, k, c * 128:(c + 1) * 128],
                                       (res_h, res_l)[b][:, u.j % RES_SLOTS, k, h * NHALF:(h + 1) * NHALF],
                                       start=(k == 0 and p == 0), stop=False)
                    for q in range(KE // 2):
                        wait_for(pe, g2_h_done, u, 2, 1 + q)
                        wait_for(pe, g2_l_done, u, 2, 1 + q)
                        for c in range(KC):
                            for h in range(2):
                                for k in (2 * q, 2 * q + 1):
                                    for p, (a, b) in enumerate(((0, 0), (1, 0), (0, 1))):
                                        last = mm(pair_a[c][:, h, 0:NHALF], w2_hl[a][:, k, c * 128:(c + 1) * 128],
                                                  (g2_h, g2_l)[b][:, k, h * NHALF:(h + 1) * NHALF],
                                                  start=False, stop=(k == KE - 1 and p == 2))
                            if q == KE // 2 - 1:
                                last.then_inc(out_ready, 1)

            run_ticks(pe, tick)

        @block.scalar
        def _(act):
            activation = nc.scalar.activation

            act.wait_ge(bn_step, 1)
            activation(bn[:, 1, :], bn[:, 0, :], ACT.Sqrt).then_inc(root_done, 1)

            def tick(t):
                if t.exists:
                    if t.known and t.image == 0 and t.j == 0:
                        act.wait_ge(bn_step, BN_STEPS)
                    wait_slot(act, x_loaded[t.j % 2], t, 2, 1)
                    for k in range(KC):
                        a = x_sb[:, t.j % 2, k, :]
                        activation(a, a, ACT.Identity, bias=bn_col(shift_x, k),
                                   scale=bn_col(gain_x, k)).then_inc(resa_done, 1)
                u = t.back(3)
                if u.exists:
                    wait_for(act, conv_step, u, CONV_STEPS, CONV_STEPS)
                    for k in range(KC):
                        g = acc[:, u.j % 2, k, :]
                        activation(g, g, ACT.Gelu).then_inc(gelu1_done, 1)
                    wait_for(act, gelu1_done, u, 2, 2)
                    wait_for(act, f1_ready, u.back(1), 4, 4)
                    activation(g1_h[:, :, :], acc[:, u.j % 2, :, :], ACT.Copy).then_inc(g1_h_done, 1)
                s = t.back(1)
                if s.exists:
                    here, before, after = (t1_sb[:, (s.j + d) % T1_SLOTS] for d in (0, -1, 1))
                    if s.known and s.image == 0 and s.j == 0:
                        act.wait_ge(made, 3)
                        act.wait_ge(kept, 4)
                    for k in range(KC):
                        wait_for(act, t1_ready, s, 2, 1 + k)
                        activation(here[:, k, 1:1 + ROWS, 1:1 + W].rearrange("p (h r) w -> p h r w", h=2),
                                   area[t.j % 2][k][:, :, 0:NHALF].rearrange("p h (r w) -> p h r w", w=W),
                                   ACT.Identity, bias=v("pi_b", k)).then_inc(t1_taken, 1)
                    for k in range(KC):
                        activation(before[:, k, T1_ROWS - 1, 1:1 + W], area[t.j % 2][k][:, 0, 0:W],
                                   ACT.Identity, bias=v("pi_b", k)).then_inc(t1_taken, 1)
                        activation(after[:, k, 0, 1:1 + W], area[t.j % 2][k][:, 1, NHALF - W:NHALF],
                                   ACT.Identity, bias=v("pi_b", k)).then_inc(t1_taken, 1)
                    wait_for(act, g1_l_done, s.back(2), 1, 1)
                    for k in range(KC):
                        activation(banks(acc[:, s.j % 2, k, :]), area[t.j % 2][k][:, :, 0:NHALF], ACT.Identity,
                                   bias=bn_col(centre_b, k), scale=tap_w(0, 0, k)).then_inc(t1_taken, 1)
                if t.exists:
                    wait_for(act, res2_done, t, 4, 4)
                    wait_for(act, out_ready, t.back(RES_SLOTS), 2, 2)
                    activation(res_h[:, t.j % RES_SLOTS], x_sb[:, t.j % 2, :, :],
                               ACT.Copy).then_inc(res_h_done, 1)
                if u.exists:
                    for q in range(KE // 2):
                        wait_for(act, g2_l_done, u, 2, q)
                        for i in range(2):
                            c = 2 * q + i
                            wait_for(act, f1_ready, u, 4, 1 + c)
                            activation(banks(g2_sb[:, i, :]),
                                       area[(t.j + q) % 2][i][:, :, 0:NHALF], ACT.Gelu,
                                       bias=b1[:, c:c + 1]).then_inc(gelu2_done, 1)
                        wait_for(act, gelu2_done, u, 4, 2 + 2 * q)
                        if q == 0:
                            wait_for(act, out_ready, u.back(1), 2, 2)
                        activation(g2_h[:, 2 * q:2 * q + 2, :], g2_sb[:, :, :], ACT.Copy).then_inc(g2_h_done, 1)

            run_ticks(act, tick)

        def bn_program(dve):
            n = 0
            tt, ts, stt = nc.vector.tensor_tensor, nc.vector.tensor_scalar, nc.vector.scalar_tensor_tensor

            def step(ins):
                nonlocal n
                n += 1
                ins.then_inc(bn_step, 1)
                dve.wait_ge(bn_step, n)

            var, y, tmp, s = (bn[:, i, :] for i in (0, 1, 2, 3))
            step(ts(var, vv("var"), EPS, None, ALU.add))
            dve.wait_ge(root_done, 1)
            step(nc.vector.reciprocal(y, y))
            for _ in range(2):
                step(tt(tmp, y, y, ALU.mult))
                step(tt(tmp, tmp, var, ALU.mult))
                step(ts(tmp, tmp, -0.5, 1.5, ALU.mult, ALU.add))
                step(tt(y, y, tmp, ALU.mult))
            step(tt(s, vv("gamma"), y, ALU.mult))
            step(tt(bn[:, gain_x, :], vv("ar"), s, ALU.mult))
            step(tt(bn[:, gain_z, :], vv("ai"), s, ALU.mult))
            step(tt(tmp, vv("mean"), s, ALU.mult))
            step(tt(tmp, vv("beta"), tmp, ALU.subtract))
            step(tt(bn[:, shift_x, :], vv("ar"), tmp, ALU.mult))
            for k in range(KC):
                step(stt(bn_col(centre_b, k), v("pi_b", k), tap_w(0, 0, k), v("dw_b", k), ALU.mult, ALU.add))
            return n

        @block.vector
        def _(dve):
            tt, stt, copy = nc.vector.tensor_tensor, nc.vector.scalar_tensor_tensor, nc.vector.tensor_copy

            dve.wait_ge(vecs_loaded, 16)
            assert bn_program(dve) == BN_STEPS

            splits = [0]

            def split(hl, src):
                copy(hl[0], src).then_inc(split_h, 1)
                splits[0] += 1
                dve.wait_ge(split_h, splits[0])
                return tt(hl[1], src, hl[0].bitcast(f32), ALU.subtract)

            dve.wait_ge(made, 1)
            copy(r_p, area[0][0][:, :, 0:C]).then_inc(kept, 1)
            split([w[:, :, :] for w in pi_hl], r_pi)
            split([w[:, :, :] for w in post_hl], r_post).then_inc(kept, 1)
            dve.wait_ge(made, 2)
            split([w[:, :, :] for w in w1_hl], area[0][1][:, :, 0:E2])
            tt(b1[:, :], area[1][0][:, 0, 0:2 * KE].rearrange("p (o two) -> p o two", two=2)[:, :, 0],
               vecs[:, VEC["ffn1_b"]:VEC["ffn1_b"] + KE], ALU.add).then_inc(kept, 1)
            dve.wait_ge(made, 3)
            split([w[:, :, :].rearrange("p (a b) n -> p a (b n)", a=2) for w in w2_hl], area[1][1][:, :, :])
            tt(b_out[:, :], area[1][0][:, 1, 0:2 * KC].rearrange("p (o two) -> p o two", two=2)[:, :, 0],
               vv("post_b"), ALU.add).then_inc(kept, 1)
            dve.wait_ge(pads_zeroed, 1)

            def tick(t):
                o = t.back(4)
                if o.exists:
                    wait_slot(dve, xres_loaded[o.j % 2], o, 2, 1)
                    for k in range(KC):
                        wait_for(dve, out_ready, o, 2, 1 + k)
                        y = banks(xres_sb[:, o.j % 2, k, :])
                        stt(y, area[(t.j - 1) % 2][k][:, :, 0:NHALF], b_out[:, k:k + 1], y,
                            ALU.add, ALU.add).then_inc(out_added, 1)
                u = t.back(3)
                if u.exists:
                    wait_for(dve, g1_h_done, u, 1, 1)
                    tt(g1_l[:, :, :], acc[:, u.j % 2, :, :], g1_h[:, :, :].bitcast(f32),
                       ALU.subtract).then_inc(g1_l_done, 1)
                w = t.back(2)

                def taps(first, last):
                    if not w.exists:
                        return
                    for i in range(first, last):
                        dh, dw = TAPS[i]
                        lo = 1 if w.j == 0 and dh == -1 else 0
                        hi = ROWS - 1 if w.j == TPI - 1 and dh == 1 else ROWS
                        if i == 0:
                            wait_for(dve, t1_taken, w, 8, 8)
                        if dh == 1 and w.j != TPI - 1:
                            wait_for(dve, t1_taken, w.back(-1), 8, 6)
                        for k in range(KC):
                            if i > 0:
                                wait_for(dve, conv_step, w, CONV_STEPS, KC * (i - 1) + k + 1)
                            src = t1_sb[:, w.j % T1_SLOTS, k, 1 + lo + dh:1 + hi + dh, 1 + dw:1 + dw + W]
                            a = image_rows(acc[:, w.j % 2, k, :])[:, lo:hi, :]
                            stt(a, src, tap_w(dh, dw, k), a, ALU.mult, ALU.add).then_inc(conv_step, 1)

                def split_g2(q):
                    if not u.exists:
                        return
                    wait_for(dve, g2_h_done, u, 2, 1 + q)
                    tt(g2_l[:, 2 * q:2 * q + 2, :], g2_sb[:, :, :], g2_h[:, 2 * q:2 * q + 2, :].bitcast(f32),
                       ALU.subtract).then_inc(g2_l_done, 1)

                taps(0, 2)
                if t.exists:
                    wait_for(dve, resa_done, t, 2, 2)
                    for k in range(KC):
                        wait_for(dve, z_done, t, 2, 1 + k)
                        z = area[1 - t.j % 2][k][:, :, :].rearrange("p h n -> p (h n)")[:, 0:ROWS * Z_ROW]
                        z = z.rearrange("p (r n) -> p r n", n=Z_ROW)
                        for e in range(2):
                            y = image_rows(x_sb[:, t.j % 2, k, :])[:, :, 1 - e:W:2]
                            stt(y, z[:, :, e * HW:(e + 1) * HW], bn_col(gain_z, k), y,
                                ALU.mult, ALU.add).then_inc(res2_done, 1)
                taps(2, 5)
                split_g2(0)
                taps(5, 6)
                split_g2(1)
                taps(6, 8)

            run_ticks(dve, tick)

        @block.gpsimd
        def _(pool):
            pool.wait_ge(made, 3)
            pool.wait_ge(kept, 4)
            t1_all = t1_sb[:, :, :, :, :].rearrange("p s k r w -> p (s k r) w")
            nc.gpsimd.memset(t1_all[:, :, 0:T1_COLS:T1_COLS - 1], 0.0).then_inc(pads_zeroed, 1)

            def tick(t):
                if t.exists:
                    wait_for(pool, res_h_done, t, 1, 1)
                    nc.gpsimd.tensor_tensor(res_l[:, t.j % RES_SLOTS], x_sb[:, t.j % 2, :, :],
                                            res_h[:, t.j % RES_SLOTS].bitcast(f32),
                                            ALU.subtract).then_inc(res_l_done, 1)

            run_ticks(pool, tick)


def kernel(**inputs):
    import numpy as _np
    import concourse.bacc as _bacc
    from concourse import mybir as _mybir
    from concourse.bass_utils import run_bass_kernel_spmd as _run

    a = {k.replace("L0_conv_", ""): _np.asarray(i) for k, i in inputs.items()}

    def by_partition(vector):
        return vector.reshape(-1, 128).T

    vec = _np.concatenate(
        [by_partition(a[n]) for n in ("bn_gamma", "bn_beta", "bn_mean", "bn_var")]
        + [by_partition(a["alpha_real"].reshape(-1)), by_partition(a["alpha_imag"].reshape(-1))]
        + [by_partition(a[n]) for n in ("pi_b", "dw_b", "fpw_b", "ffn2_b", "po_b", "post_b", "ffn1_b")]
        + [a["dw_w"].reshape(KC, 128, 9).transpose(1, 0, 2).reshape(128, KC * 9)], axis=1)
    d = _np.arange(W)[None, :] - _np.arange(W)[:, None]
    odd = d % 2 != 0
    toep = _np.where(odd, -(2.0 / W) / _np.tan(_np.pi * _np.where(odd, d, 1) / W), 0.0).astype(_np.float32)
    toep1 = _np.concatenate([toep[:, 1::2], toep[:, 0::2]], axis=1)
    toep3 = _np.zeros((GROUP, HW, 2, GROUP, HW), _np.float32)
    for r in range(GROUP):
        for e in range(2):
            toep3[r, :, e, r, :] = toep[e::2, 1 - e::2]
    rows = a["x"].reshape(B, C, TPI, ROWS, HW, 2)
    xw3 = rows[:, :, :, :ROWS - 1].reshape(B, C, TPI, GROUPS, GROUP, HW, 2).transpose(0, 2, 4, 5, 3, 6, 1)
    xw1 = rows[:, :, :, ROWS - 1].transpose(0, 2, 3, 4, 1)

    arrays = {
        "x": a["x"], "xw3": xw3.reshape(B, TPI, GROUP * HW, GROUPS * 2, C), "xw1": xw1.reshape(B, TPI, W, C), "vec": vec,
        "toep3": toep3.reshape(GROUP * HW, 2, GROUP * HW), "toep1": toep1,
        "pi_t": a["pi_w"].T, "fpw": a["fpw_w"], "ffn1_t": a["ffn1_w"].T, "ffn2": a["ffn2_w"],
        "po": a["po_w"], "post_t": a["post_w"].T,
    }
    arrays = {k: _np.ascontiguousarray(i) for k, i in arrays.items()}
    nc = _bacc.Bacc("TRN2", target_bir_lowering=False, num_devices=1)
    args = [nc.dram_tensor(f"in_{k}", i.shape, _mybir.dt.from_np(i.dtype), kind="ExternalInput").ap()
            for k, i in arrays.items()]
    out = nc.dram_tensor("out_0", (B, C, H, W), _mybir.dt.float32, kind="ExternalOutput").ap()
    conv_block_program(nc, *args, out)
    r = _run(nc, [{f"in_{k}": i for k, i in arrays.items()}], core_ids=[0])
    return r.results[0]["out_0"]
```

```python
import concourse.bass as bass
from concourse import mybir
from contextlib import ExitStack

B, C, H, W = 8, 256, 80, 80
E2 = 2 * C
KC = C // 128
KE = E2 // 128
ROWS = 10
HALF = ROWS // 2
NPX = ROWS * W
NHALF = HALF * W
TPI = H // ROWS
TILES = B * TPI
LAST_LAG = 4
HW = W // 2
GROUP = 3
GROUPS = ROWS // GROUP
assert GROUPS * GROUP == ROWS - 1
Z_ROW = 86
assert all((r * Z_ROW) // 512 == (r * Z_ROW + W - 1) // 512 for r in range(ROWS))
assert all((g * GROUP * Z_ROW) // 512 == ((g * GROUP + GROUP - 1) * Z_ROW) // 512 for g in range(GROUPS))
T1_SLOTS = 4
T1_ROWS, T1_COLS = ROWS + 2, W + 2
RES_SLOTS = 4
TAPS = [(0, -1), (0, 1), (-1, -1), (-1, 0), (-1, 1), (1, -1), (1, 0), (1, 1)]
CONV_STEPS = KC * len(TAPS)
EPS = 1e-5
BN_STEPS = 2 + 2 * 4 + 6 + KC
VEC = {n: KC * i for i, n in enumerate(
    ["gamma", "beta", "mean", "var", "ar", "ai", "pi_b", "dw_b", "fpw_b", "ffn2_b", "po_b", "post_b"])}
VEC["ffn1_b"] = KC * 12
VEC["dw_w"] = VEC["ffn1_b"] + KE
NVEC = VEC["dw_w"] + 9 * KC


class Tile:

    def __init__(self, image, j):
        self.image, self.j = image, j

    def back(self, lag):
        j = self.j - lag
        return Tile(self.image + j // TPI, j % TPI) if j // TPI else Tile(self.image, j)

    @property
    def known(self):
        return isinstance(self.image, int)

    def is_number(self, n):
        return self.known and self.image * TPI + self.j == n

    @property
    def exists(self):
        return not self.known or 0 <= self.image * TPI + self.j < TILES

    def count(self, per_tile, more=0):
        return self.image * (TPI * per_tile) + (self.j * per_tile + more)

    def slot_count(self, slots, more=0, by=16):
        return self.image * (by * TPI // slots) + by * (self.j // slots + more)


def wait_for(eng, sem, tile, per_tile, more):
    if tile.exists and (not tile.known or tile.count(per_tile, more) > 0):
        eng.wait_ge(sem, tile.count(per_tile, more))


def wait_slot(eng, sem, tile, slots, more, by=16):
    if tile.exists and (not tile.known or tile.slot_count(slots, more, by) > 0):
        eng.wait_ge(sem, tile.slot_count(slots, more, by))


def run_ticks(eng, tick):
    for j in range(TPI):
        tick(Tile(0, j))
    with eng.Fori(1, B) as image:
        for j in range(TPI):
            tick(Tile(image, j))
    for j in range(LAST_LAG):
        tick(Tile(B, j))


def conv_block_program(nc, x, xw3, xw1, vec, toep, raw_a, raw_b, out):
    f32 = mybir.dt.float32
    f32r = mybir.dt.float32r
    ALU = mybir.AluOpType
    ACT = mybir.ActivationFunctionType

    x_v = x.rearrange("b (k p) (j r) w -> b j p k (r w)", p=128, r=ROWS)
    out_v = out.rearrange("b (k p) (j r) w -> b j p k (r w)", p=128, r=ROWS)

    ctx = ExitStack()
    with ctx:
        def sb(name, shape, dt=f32):
            return ctx.enter_context(nc.sbuf_tensor(name, shape, dt))

        def sem(name):
            return ctx.enter_context(nc.semaphore(name))

        pi_hl = [sb(f"pi_{s}", [128, KC, C], f32r) for s in "hl"]
        post_hl = [sb(f"post_{s}", [128, KC, C], f32r) for s in "hl"]
        w1_hl = [sb(f"w1_{s}", [128, KC, E2], f32r) for s in "hl"]
        w2_hl = [sb(f"w2_{s}", [128, KE, C], f32r) for s in "hl"]
        toep_sb = sb("toep_sb", [GROUP * HW, 2 * GROUP * HW + W])
        toep3_sb = toep_sb[:, 0:2 * GROUP * HW].rearrange("p (e n) -> p e n", e=2)
        toep1_sb = toep_sb[0:W, 2 * GROUP * HW:]
        vecs = sb("vecs", [128, NVEC])
        bn = sb("bn", [128, 8, KC])
        b1 = sb("b1", [128, KE])
        b_out = sb("b_out", [128, KC])

        x_sb = sb("x_sb", [128, 2, KC, NPX])
        xw3_sb = sb("xw3_sb", [GROUP * HW, 2, GROUPS * 2, C])
        xw1_sb = sb("xw1_sb", [W, 2, C])
        xres_sb = sb("xres_sb", [128, 2, KC, NPX])
        res_h = sb("res_h", [128, RES_SLOTS, KC, NPX], f32r)
        res_l = sb("res_l", [128, RES_SLOTS, KC, NPX], f32r)
        t1_sb = sb("t1_sb", [128, T1_SLOTS, KC, T1_ROWS, T1_COLS])
        acc = sb("acc", [128, 2, KC, NPX])
        g1_h = sb("g1_h", [128, KC, NPX], f32r)
        g1_l = sb("g1_l", [128, KC, NPX], f32r)
        g2_sb = sb("g2_sb", [128, 2, NPX])
        g2_h = sb("g2_h", [128, KE, NPX], f32r)
        g2_l = sb("g2_l", [128, KE, NPX], f32r)
        area = [[ctx.enter_context(nc.psum_tensor(f"area_{p}{c}", [128, 2, 512], f32)) for c in range(2)]
                for p in range(2)]

        def raw_views(ap, sizes):
            views, at = [], 0
            for chunks, n in sizes:
                views.append(ap[:, at:at + chunks * n].rearrange("p (k n) -> p k n", k=chunks))
                at += chunks * n
            return views

        xres_flat = xres_sb[:, :, :, :].rearrange("p s k n -> p (s k n)")
        g2_flat = g2_sb[:, :, :].rearrange("p k n -> p (k n)")
        r_post, r_po, r_ffn2, r_fpw, r_p = raw_views(
            xres_flat, [(KC, C), (KC, C), (KC, E2), (KC, C), (KC, C)])
        r_pi, r_ffn1 = raw_views(g2_flat, [(KC, C), (KC, E2)])

        vecs_loaded, toep_loaded = sem("vecs_loaded"), sem("toep_loaded")
        raw_a_loaded, raw_b_loaded = sem("raw_a_loaded"), sem("raw_b_loaded")
        x_loaded = [sem(f"x_loaded{i}") for i in range(2)]
        xw_loaded = [sem(f"xw_loaded{i}") for i in range(2)]
        xres_loaded = [sem(f"xres_loaded{i}") for i in range(2)]
        out_stored = [sem(f"out_stored{i}") for i in range(2)]
        bn_step = sem("bn_step")
        root_done = sem("root_done")
        made = sem("made")
        w_copied = sem("w_copied")
        w_split = sem("w_split")
        pads_zeroed = sem("pads_zeroed")
        z_done = sem("z_done")
        resa_done = sem("resa_done")
        res2_done = sem("res2_done")
        res_h_done = sem("res_h_done")
        res_l_done = sem("res_l_done")
        t1_ready = sem("t1_ready")
        t1_taken = sem("t1_taken")
        conv_step = sem("conv_step")
        gelu1_done = sem("gelu1_done")
        g1_h_done = sem("g1_h_done")
        g1_l_done = sem("g1_l_done")
        f1_ready = sem("f1_ready")
        gelu2_done = sem("gelu2_done")
        g2_h_done = sem("g2_h_done")
        g2_l_done = sem("g2_l_done")
        out_ready = sem("out_ready")
        out_added = sem("out_added")

        def v(name, k):
            return vecs[:, VEC[name] + k:VEC[name] + k + 1]

        def vv(name):
            return vecs[:, VEC[name]:VEC[name] + KC]

        gain_x, shift_x, gain_z, centre_b = 4, 5, 6, 7

        def bn_col(row, k):
            return bn[:, row, k:k + 1]

        def tap_w(dh, dw, k):
            i = VEC["dw_w"] + 9 * k + 3 * (dh + 1) + (dw + 1)
            return vecs[:, i:i + 1]

        def banks(ap):
            return ap.rearrange("p (h n) -> p h n", h=2)

        def image_rows(ap):
            return ap.rearrange("p (r w) -> p r w", w=W)

        block = ctx.enter_context(nc.Block())

        @block.sync
        def _(sp):
            def load_xres(r):
                sp.dma_start(xres_sb[:, r.j % 2, :, :], x_v[r.image, r.j]).then_inc(xres_loaded[r.j % 2], 16)

            sp.dma_start(vecs[:, :], vec).then_inc(vecs_loaded, 16)
            sp.dma_start(toep_sb[:, :], toep).then_inc(toep_loaded, 16)

            def tick(t):
                if t.exists:
                    wait_for(sp, z_done, t.back(2), 2, 2)
                    sp.dma_start(xw3_sb[:, t.j % 2, :, :], xw3[t.image, t.j]).then_inc(xw_loaded[t.j % 2], 16)
                    sp.dma_start(xw1_sb[:, t.j % 2, :], xw1[t.image, t.j]).then_inc(xw_loaded[t.j % 2], 16)
                    wait_for(sp, res_l_done, t.back(2), 1, 1)
                    sp.dma_start(x_sb[:, t.j % 2, :, :], x_v[t.image, t.j]).then_inc(x_loaded[t.j % 2], 16)
                o = t.back(LAST_LAG)
                if o.exists:
                    wait_for(sp, out_added, o, 2, 2)
                    sp.dma_start(out_v[o.image, o.j], xres_sb[:, o.j % 2, :, :]).then_inc(out_stored[o.j % 2], 16)
                r = t.back(LAST_LAG - 2)
                if t.is_number(3):
                    sp.wait_ge(made, 3)
                    load_xres(r.back(1))
                if r.exists and not r.is_number(0):
                    wait_slot(sp, out_stored[r.j % 2], r, 2, 0)
                    load_xres(r)

            run_ticks(sp, tick)
            for s in range(2):
                sp.wait_ge(out_stored[s], 16 * TILES // 2)

        @block.tensor
        def _(pe):
            mm = nc.tensor.matmul

            def products(pairs, dst, stat, mov):
                n = len(pairs)
                for i, (ws, ms) in enumerate(pairs):
                    for p, (a, b) in enumerate(((0, 0), (1, 0), (0, 1))):
                        last = mm(dst, ws(stat[a]), ms(mov[b]), start=(i == 0 and p == 0),
                                  stop=(i == n - 1 and p == 2))
                return last

            def weight_products():
                pe.wait_ge(raw_a_loaded, 16)
                pe.wait_ge(raw_b_loaded, 16)
                pe.wait_ge(t1_taken, 16)
                for k in range(KC):
                    for q in range(KC):
                        last = mm(area[0][0][:, 0, k * C:(k + 1) * C], r_po[:, q, k * 128:(k + 1) * 128],
                                  r_post[:, q, :], start=(q == 0), stop=(q == KC - 1))
                last.then_inc(made, 1)
                for o in range(KE):
                    for q in range(KC):
                        mm(area[0][0][:, 1, 2 * o:2 * o + 1], r_ffn1[:, q, o * 128:(o + 1) * 128],
                           v("fpw_b", q), start=(q == 0), stop=(q == KC - 1))
                for k in range(KC):
                    for q in range(KC):
                        last = mm(area[0][1][:, k, 0:E2], r_fpw[:, q, k * 128:(k + 1) * 128], r_ffn1[:, q, :],
                                  start=(q == 0), stop=(q == KC - 1))
                last.then_inc(made, 1)
                pe.wait_ge(w_copied, 1)
                pe.wait_ge(res2_done, 12)
                for o in range(KC):
                    for i, (w, b) in enumerate(((r_p, "ffn2_b"), (r_post, "po_b"))):
                        for q in range(KC):
                            mm(area[1][0][:, 1, 2 * o:2 * o + 1], w[:, q, o * 128:(o + 1) * 128], v(b, q),
                               start=(i == 0 and q == 0), stop=(i == 1 and q == KC - 1))
                for k in range(KE):
                    for q in range(KC):
                        last = mm(area[1][1][:, k // 2, (k % 2) * C:(k % 2 + 1) * C],
                                  r_ffn2[:, q, k * 128:(k + 1) * 128], r_p[:, q, :],
                                  start=(q == 0), stop=(q == KC - 1))
                last.then_inc(made, 1)

            def t1_stage(s, t, pair_a):
                if s.exists:
                    if s.is_number(0):
                        pe.wait_ge(w_split, 2)
                    if s.is_number(2):
                        pe.wait_ge(w_copied, 3)
                        pe.wait_ge(w_split, 8)
                    wait_for(pe, res_h_done, s, 1, 1)
                    wait_for(pe, res_l_done, s, 1, 1)
                    for c in range(KC):
                        wait_for(pe, gelu2_done, t.back(4), 4, 3 + c)
                        for h in range(2):
                            pairs = [(lambda w, k=k: w[:, k, c * 128:(c + 1) * 128],
                                      lambda m, k=k: m[:, s.j % RES_SLOTS, k, h * NHALF:(h + 1) * NHALF])
                                     for k in range(KC)]
                            last = products(pairs, pair_a[c][:, h, 0:NHALF], pi_hl, (res_h, res_l))
                        last.then_inc(t1_ready, 1)

            def z_stage(t, pair_b):
                if t.exists:
                    if t.is_number(0):
                        pe.wait_ge(toep_loaded, 16)
                    if t.is_number(3):
                        pe.wait_ge(w_split, 6)
                    if t.back(4).exists:
                        wait_for(pe, out_added, t.back(4), 2, 2)
                    else:
                        wait_for(pe, t1_taken, t.back(2), 8, 8)
                    wait_slot(pe, xw_loaded[t.j % 2], t, 2, 1, 32)
                    for c in range(KC):
                        z = pair_b[c][:, :, :].rearrange("p h n -> p (h n)")
                        for g in range(GROUPS):
                            for e in range(2):
                                rows = z[:, g * GROUP * Z_ROW:(g + 1) * GROUP * Z_ROW]
                                mm(rows.rearrange("p (r n) -> p r n", n=Z_ROW)[:, :, e * HW:(e + 1) * HW],
                                   xw3_sb[:, t.j % 2, 2 * g + e, c * 128:(c + 1) * 128], toep3_sb[:, e, :],
                                   start=True, stop=True)
                        mm(z[:, (ROWS - 1) * Z_ROW:(ROWS - 1) * Z_ROW + W],
                           xw1_sb[:, t.j % 2, c * 128:(c + 1) * 128], toep1_sb,
                           start=True, stop=True).then_inc(z_done, 1)

            def tick(t):
                pair_a, pair_b = area[t.j % 2], area[1 - t.j % 2]
                s, u = t.back(1), t.back(3)
                if t.is_number(1):
                    z_stage(t, pair_b)
                    t1_stage(s, t, pair_a)
                else:
                    t1_stage(s, t, pair_a)
                    z_stage(t, pair_b)
                if t.is_number(2):
                    weight_products()
                if u.exists:
                    wait_for(pe, g1_h_done, u, 1, 1)
                    wait_for(pe, g1_l_done, u, 1, 1)
                    for c in range(KE):
                        dst = (pair_a, pair_b)[c // 2][c % 2]
                        if c < 2:
                            if s.exists:
                                wait_for(pe, t1_taken, s, 8, 7 + c)
                            else:
                                wait_for(pe, gelu2_done, t.back(4), 4, 3 + c)
                        else:
                            if t.exists:
                                wait_for(pe, res2_done, t, 4, 2 * (c - 1))
                            else:
                                wait_for(pe, out_added, t.back(4), 2, c - 1)
                        for h in range(2):
                            pairs = [(lambda w, k=k: w[:, k, c * 128:(c + 1) * 128],
                                      lambda m, k=k: m[:, k, h * NHALF:(h + 1) * NHALF]) for k in range(KC)]
                            last = products(pairs, dst[:, h, 0:NHALF], w1_hl, (g1_h, g1_l))
                        last.then_inc(f1_ready, 1)
                    for c in range(KC):
                        wait_for(pe, gelu2_done, u, 4, 1 + c)
                        for h in range(2):
                            for k in range(KC):
                                for p, (a, b) in enumerate(((0, 0), (1, 0), (0, 1))):
                                    mm(pair_a[c][:, h, 0:NHALF], post_hl[a][:, k, c * 128:(c + 1) * 128],
                                       (res_h, res_l)[b][:, u.j % RES_SLOTS, k, h * NHALF:(h + 1) * NHALF],
                                       start=(k == 0 and p == 0), stop=False)
                    for q in range(KE // 2):
                        wait_for(pe, g2_h_done, u, 2, 1 + q)
                        wait_for(pe, g2_l_done, u, 2, 1 + q)
                        for c in range(KC):
                            for h in range(2):
                                for k in (2 * q, 2 * q + 1):
                                    for p, (a, b) in enumerate(((0, 0), (1, 0), (0, 1))):
                                        last = mm(pair_a[c][:, h, 0:NHALF], w2_hl[a][:, k, c * 128:(c + 1) * 128],
                                                  (g2_h, g2_l)[b][:, k, h * NHALF:(h + 1) * NHALF],
                                                  start=False, stop=(k == KE - 1 and p == 2))
                            if q == KE // 2 - 1:
                                last.then_inc(out_ready, 1)

            run_ticks(pe, tick)

        @block.scalar
        def _(act):
            activation = nc.scalar.activation

            act.wait_ge(bn_step, 1)
            activation(bn[:, 1, :], bn[:, 0, :], ACT.Sqrt).then_inc(root_done, 1)
            act.dma_start(g2_flat[:, 0:raw_b.shape[1]], raw_b).then_inc(raw_b_loaded, 16)
            act.dma_start(xres_flat[:, 0:raw_a.shape[1]], raw_a).then_inc(raw_a_loaded, 16)

            def copy_weights():
                act.wait_ge(made, 1)
                activation(r_p, area[0][0][:, 0, :].rearrange("p (k n) -> p k n", k=KC),
                           ACT.Copy).then_inc(w_copied, 1)
                act.wait_ge(made, 2)
                activation(w1_hl[0][:, :, :], area[0][1][:, :, :], ACT.Copy).then_inc(w_copied, 1)
                act.wait_ge(made, 3)
                activation(w2_hl[0][:, :, :].rearrange("p (a b) n -> p a (b n)", a=2), area[1][1][:, :, :],
                           ACT.Copy).then_inc(w_copied, 1)

            def res_h_stage(t):
                if t.exists:
                    wait_for(act, res2_done, t, 4, 4)
                    wait_for(act, out_ready, t.back(RES_SLOTS), 2, 2)
                    activation(res_h[:, t.j % RES_SLOTS], x_sb[:, t.j % 2, :, :],
                               ACT.Copy).then_inc(res_h_done, 1)

            def tick(t):
                if t.exists:
                    if t.is_number(0):
                        act.wait_ge(bn_step, BN_STEPS)
                    wait_slot(act, x_loaded[t.j % 2], t, 2, 1)
                    for k in range(KC):
                        a = x_sb[:, t.j % 2, k, :]
                        activation(a, a, ACT.Identity, bias=bn_col(shift_x, k),
                                   scale=bn_col(gain_x, k)).then_inc(resa_done, 1)
                u = t.back(3)
                if u.exists:
                    wait_for(act, conv_step, u, CONV_STEPS, CONV_STEPS)
                    for k in range(KC):
                        g = acc[:, u.j % 2, k, :]
                        activation(g, g, ACT.Gelu).then_inc(gelu1_done, 1)
                    wait_for(act, gelu1_done, u, 2, 2)
                    wait_for(act, f1_ready, u.back(1), 4, 4)
                    activation(g1_h[:, :, :], acc[:, u.j % 2, :, :], ACT.Copy).then_inc(g1_h_done, 1)
                s = t.back(1)
                if t.is_number(1):
                    res_h_stage(t)
                if s.exists:
                    here, before, after = (t1_sb[:, (s.j + d) % T1_SLOTS] for d in (0, -1, 1))
                    for k in range(KC):
                        wait_for(act, t1_ready, s, 2, 1 + k)
                        activation(here[:, k, 1:1 + ROWS, 1:1 + W].rearrange("p (h r) w -> p h r w", h=2),
                                   area[t.j % 2][k][:, :, 0:NHALF].rearrange("p h (r w) -> p h r w", w=W),
                                   ACT.Identity, bias=v("pi_b", k)).then_inc(t1_taken, 1)
                    for k in range(KC):
                        activation(before[:, k, T1_ROWS - 1, 1:1 + W], area[t.j % 2][k][:, 0, 0:W],
                                   ACT.Identity, bias=v("pi_b", k)).then_inc(t1_taken, 1)
                        activation(after[:, k, 0, 1:1 + W], area[t.j % 2][k][:, 1, NHALF - W:NHALF],
                                   ACT.Identity, bias=v("pi_b", k)).then_inc(t1_taken, 1)
                    wait_for(act, g1_l_done, s.back(2), 1, 1)
                    for k in range(KC):
                        activation(banks(acc[:, s.j % 2, k, :]), area[t.j % 2][k][:, :, 0:NHALF], ACT.Identity,
                                   bias=bn_col(centre_b, k), scale=tap_w(0, 0, k)).then_inc(t1_taken, 1)
                if not t.is_number(1):
                    res_h_stage(t)
                if t.is_number(2):
                    copy_weights()
                if u.is_number(0):
                    act.wait_ge(w_split, 6)
                if u.exists:
                    for q in range(KE // 2):
                        wait_for(act, g2_l_done, u, 2, q)
                        for i in range(2):
                            c = 2 * q + i
                            wait_for(act, f1_ready, u, 4, 1 + c)
                            activation(banks(g2_sb[:, i, :]),
                                       area[(t.j + q) % 2][i][:, :, 0:NHALF], ACT.Gelu,
                                       bias=b1[:, c:c + 1]).then_inc(gelu2_done, 1)
                        wait_for(act, gelu2_done, u, 4, 2 + 2 * q)
                        if q == 0:
                            wait_for(act, out_ready, u.back(1), 2, 2)
                        activation(g2_h[:, 2 * q:2 * q + 2, :], g2_sb[:, :, :], ACT.Copy).then_inc(g2_h_done, 1)

            run_ticks(act, tick)

        def bn_program(dve):
            n = 0
            tt, ts, stt = nc.vector.tensor_tensor, nc.vector.tensor_scalar, nc.vector.scalar_tensor_tensor

            def step(ins):
                nonlocal n
                n += 1
                ins.then_inc(bn_step, 1)
                dve.wait_ge(bn_step, n)

            var, y, tmp, s = (bn[:, i, :] for i in (0, 1, 2, 3))
            step(ts(var, vv("var"), EPS, None, ALU.add))
            dve.wait_ge(root_done, 1)
            step(nc.vector.reciprocal(y, y))
            for _ in range(2):
                step(tt(tmp, y, y, ALU.mult))
                step(tt(tmp, tmp, var, ALU.mult))
                step(ts(tmp, tmp, -0.5, 1.5, ALU.mult, ALU.add))
                step(tt(y, y, tmp, ALU.mult))
            step(tt(s, vv("gamma"), y, ALU.mult))
            step(tt(bn[:, gain_x, :], vv("ar"), s, ALU.mult))
            step(tt(bn[:, gain_z, :], vv("ai"), s, ALU.mult))
            step(tt(tmp, vv("mean"), s, ALU.mult))
            step(tt(tmp, vv("beta"), tmp, ALU.subtract))
            step(tt(bn[:, shift_x, :], vv("ar"), tmp, ALU.mult))
            for k in range(KC):
                step(stt(bn_col(centre_b, k), v("pi_b", k), tap_w(0, 0, k), v("dw_b", k), ALU.mult, ALU.add))
            return n

        @block.vector
        def _(dve):
            tt, stt, copy = nc.vector.tensor_tensor, nc.vector.scalar_tensor_tensor, nc.vector.tensor_copy

            dve.wait_ge(vecs_loaded, 16)
            assert bn_program(dve) == BN_STEPS

            def split_weight(hl, raw, loaded, steps):
                dve.wait_ge(loaded, 16)
                copy(hl[0][:, :, :], raw).then_inc(w_split, 1)
                dve.wait_ge(w_split, steps + 1)
                tt(hl[1][:, :, :], raw, hl[0][:, :, :].bitcast(f32), ALU.subtract).then_inc(w_split, 1)

            dve.wait_ge(pads_zeroed, 1)

            def split_products(wn_hl, count):
                dve.wait_ge(made, count)
                dve.wait_ge(w_copied, count)
                w = [i[:, :, :].rearrange("p k n -> p (k n)").rearrange("p (a b) -> p a b", a=2) for i in wn_hl]
                pair = area[count - 2]
                tt(w[1], pair[1][:, :, :], w[0].bitcast(f32), ALU.subtract).then_inc(w_split, 1)
                bias, n, first = (b1, KE, VEC["ffn1_b"]) if count == 2 else (b_out, KC, VEC["post_b"])
                tt(bias[:, :], pair[0][:, 1, 0:2 * n].rearrange("p (o two) -> p o two", two=2)[:, :, 0],
                   vecs[:, first:first + n], ALU.add).then_inc(w_split, 1)

            def tick(t):
                o = t.back(4)
                if o.exists:
                    wait_slot(dve, xres_loaded[o.j % 2], o, 2, 1)
                    for k in range(KC):
                        wait_for(dve, out_ready, o, 2, 1 + k)
                        y = banks(xres_sb[:, o.j % 2, k, :])
                        stt(y, area[(t.j - 1) % 2][k][:, :, 0:NHALF], b_out[:, k:k + 1], y,
                            ALU.add, ALU.add).then_inc(out_added, 1)
                u = t.back(3)
                if u.exists:
                    wait_for(dve, g1_h_done, u, 1, 1)
                    tt(g1_l[:, :, :], acc[:, u.j % 2, :, :], g1_h[:, :, :].bitcast(f32),
                       ALU.subtract).then_inc(g1_l_done, 1)
                w = t.back(2)

                def taps(first, last):
                    if not w.exists:
                        return
                    for i in range(first, last):
                        dh, dw = TAPS[i]
                        lo = 1 if w.j == 0 and dh == -1 else 0
                        hi = ROWS - 1 if w.j == TPI - 1 and dh == 1 else ROWS
                        if i == 0:
                            wait_for(dve, t1_taken, w, 8, 8)
                        if dh == 1 and w.j != TPI - 1:
                            wait_for(dve, t1_taken, w.back(-1), 8, 6)
                        for k in range(KC):
                            if i > 0:
                                wait_for(dve, conv_step, w, CONV_STEPS, KC * (i - 1) + k + 1)
                            src = t1_sb[:, w.j % T1_SLOTS, k, 1 + lo + dh:1 + hi + dh, 1 + dw:1 + dw + W]
                            a = image_rows(acc[:, w.j % 2, k, :])[:, lo:hi, :]
                            stt(a, src, tap_w(dh, dw, k), a, ALU.mult, ALU.add).then_inc(conv_step, 1)

                def split_g2(q):
                    if not u.exists:
                        return
                    wait_for(dve, g2_h_done, u, 2, 1 + q)
                    tt(g2_l[:, 2 * q:2 * q + 2, :], g2_sb[:, :, :], g2_h[:, 2 * q:2 * q + 2, :].bitcast(f32),
                       ALU.subtract).then_inc(g2_l_done, 1)

                taps(0, 2)
                if t.exists:
                    wait_for(dve, resa_done, t, 2, 2)
                    for k in range(KC):
                        wait_for(dve, z_done, t, 2, 1 + k)
                        z = area[1 - t.j % 2][k][:, :, :].rearrange("p h n -> p (h n)")[:, 0:ROWS * Z_ROW]
                        z = z.rearrange("p (r n) -> p r n", n=Z_ROW)
                        for e in range(2):
                            y = image_rows(x_sb[:, t.j % 2, k, :])[:, :, 1 - e:W:2]
                            stt(y, z[:, :, e * HW:(e + 1) * HW], bn_col(gain_z, k), y,
                                ALU.mult, ALU.add).then_inc(res2_done, 1)
                taps(2, 5)
                split_g2(0)
                taps(5, 6)
                split_g2(1)
                if t.is_number(2):
                    split_products(w1_hl, 2)
                taps(6, 8)
                if t.is_number(2):
                    split_products(w2_hl, 3)
                if t.is_number(0):
                    split_weight(pi_hl, r_pi, raw_b_loaded, 0)
                if t.is_number(1):
                    split_weight(post_hl, r_post, raw_a_loaded, 2)

            run_ticks(dve, tick)

        @block.gpsimd
        def _(pool):
            t1_all = t1_sb[:, :, :, :, :].rearrange("p s k r w -> p (s k r) w")
            nc.gpsimd.memset(t1_all[:, :, 0:T1_COLS:T1_COLS - 1], 0.0).then_inc(pads_zeroed, 1)

            def tick(t):
                if t.exists:
                    wait_for(pool, res_h_done, t, 1, 1)
                    nc.gpsimd.tensor_tensor(res_l[:, t.j % RES_SLOTS], x_sb[:, t.j % 2, :, :],
                                            res_h[:, t.j % RES_SLOTS].bitcast(f32),
                                            ALU.subtract).then_inc(res_l_done, 1)

            run_ticks(pool, tick)


def kernel(**inputs):
    import numpy as _np
    import concourse.bacc as _bacc
    from concourse import mybir as _mybir
    from concourse.bass_utils import run_bass_kernel_spmd as _run

    a = {k.replace("L0_conv_", ""): _np.asarray(i) for k, i in inputs.items()}

    def by_partition(vector):
        return vector.reshape(-1, 128).T

    def by_rows(matrix):
        return matrix.reshape(-1, 128, matrix.shape[1]).transpose(1, 0, 2).reshape(128, -1)

    vec = _np.concatenate(
        [by_partition(a[n]) for n in ("bn_gamma", "bn_beta", "bn_mean", "bn_var")]
        + [by_partition(a["alpha_real"].reshape(-1)), by_partition(a["alpha_imag"].reshape(-1))]
        + [by_partition(a[n]) for n in ("pi_b", "dw_b", "fpw_b", "ffn2_b", "po_b", "post_b", "ffn1_b")]
        + [a["dw_w"].reshape(KC, 128, 9).transpose(1, 0, 2).reshape(128, KC * 9)], axis=1)
    d = _np.arange(W)[None, :] - _np.arange(W)[:, None]
    odd = d % 2 != 0
    toep = _np.where(odd, -(2.0 / W) / _np.tan(_np.pi * _np.where(odd, d, 1) / W), 0.0).astype(_np.float32)
    toep1 = _np.concatenate([toep[:, 1::2], toep[:, 0::2]], axis=1)
    toep3 = _np.zeros((GROUP, HW, 2, GROUP, HW), _np.float32)
    for r in range(GROUP):
        for e in range(2):
            toep3[r, :, e, r, :] = toep[e::2, 1 - e::2]
    rows = a["x"].reshape(B, C, TPI, ROWS, HW, 2)
    xw3 = rows[:, :, :, :ROWS - 1].reshape(B, C, TPI, GROUPS, GROUP, HW, 2).transpose(0, 2, 4, 5, 3, 6, 1)
    xw1 = rows[:, :, :, ROWS - 1].transpose(0, 2, 3, 4, 1)

    arrays = {
        "x": a["x"], "xw3": xw3.reshape(B, TPI, GROUP * HW, GROUPS * 2, C), "xw1": xw1.reshape(B, TPI, W, C), "vec": vec,
        "toep": _np.concatenate([toep3.reshape(GROUP * HW, 2 * GROUP * HW),
                                 _np.pad(toep1, ((0, GROUP * HW - W), (0, 0)))], axis=1),
        "raw_a": _np.concatenate([by_rows(a["post_w"].T), by_rows(a["po_w"]), by_rows(a["ffn2_w"]),
                                  by_rows(a["fpw_w"])], axis=1),
        "raw_b": _np.concatenate([by_rows(a["pi_w"].T), by_rows(a["ffn1_w"].T)], axis=1),
    }
    arrays = {k: _np.ascontiguousarray(i) for k, i in arrays.items()}
    nc = _bacc.Bacc("TRN2", target_bir_lowering=False, num_devices=1)
    args = [nc.dram_tensor(f"in_{k}", i.shape, _mybir.dt.from_np(i.dtype), kind="ExternalInput").ap()
            for k, i in arrays.items()]
    out = nc.dram_tensor("out_0", (B, C, H, W), _mybir.dt.float32, kind="ExternalOutput").ap()
    conv_block_program(nc, *args, out)
    r = _run(nc, [{f"in_{k}": i for k, i in arrays.items()}], core_ids=[0])
    return r.results[0]["out_0"]
```

```python
import concourse.bass as bass
from concourse import mybir
from contextlib import ExitStack

B, C, H, W = 8, 256, 80, 80
E2 = 2 * C
KC = C // 128
KE = E2 // 128
ROWS = 10
HALF = ROWS // 2
NPX = ROWS * W
NHALF = HALF * W
TPI = H // ROWS
TILES = B * TPI
LAST_LAG = 4
HW = W // 2
GROUP = 3
GROUPS = ROWS // GROUP
assert GROUPS * GROUP == ROWS - 1
Z_ROW = 86
assert all((r * Z_ROW) // 512 == (r * Z_ROW + W - 1) // 512 for r in range(ROWS))
assert all((g * GROUP * Z_ROW) // 512 == ((g * GROUP + GROUP - 1) * Z_ROW) // 512 for g in range(GROUPS))
T1_SLOTS = 4
T1_ROWS, T1_COLS = ROWS + 2, W + 2
RES_SLOTS = 4
TAPS = [(0, -1), (0, 1), (-1, -1), (-1, 0), (-1, 1), (1, -1), (1, 0), (1, 1)]
CONV_STEPS = KC * len(TAPS)
PASSES = [(0, 0), (1, 0), (0, 1)]
EPS = 1e-5
BN_STEPS = 2 + 2 * 4 + 6 + KC
VEC = {n: KC * i for i, n in enumerate(
    ["gamma", "beta", "mean", "var", "ar", "ai", "pi_b", "dw_b", "fpw_b", "ffn2_b", "po_b", "post_b"])}
VEC["ffn1_b"] = KC * 12
VEC["dw_w"] = VEC["ffn1_b"] + KE
NVEC = VEC["dw_w"] + 9 * KC


class Tile:

    def __init__(self, image, j):
        self.image, self.j = image, j

    def back(self, lag):
        j = self.j - lag
        return Tile(self.image + j // TPI, j % TPI) if j // TPI else Tile(self.image, j)

    @property
    def known(self):
        return isinstance(self.image, int)

    def is_number(self, n):
        return self.known and self.image * TPI + self.j == n

    @property
    def exists(self):
        return not self.known or 0 <= self.image * TPI + self.j < TILES

    def count(self, per_tile, more=0):
        return self.image * (TPI * per_tile) + (self.j * per_tile + more)

    def slot_count(self, slots, more=0, by=16):
        return self.image * (by * TPI // slots) + by * (self.j // slots + more)


def wait_for(eng, sem, tile, per_tile, more):
    if tile.exists and (not tile.known or tile.count(per_tile, more) > 0):
        eng.wait_ge(sem, tile.count(per_tile, more))


def wait_slot(eng, sem, tile, slots, more, by=16):
    if tile.exists and (not tile.known or tile.slot_count(slots, more, by) > 0):
        eng.wait_ge(sem, tile.slot_count(slots, more, by))


def t1_pair(t):
    return t.j % 2


def z_pair(t):
    return 1 - t.j % 2


def w1_pair(t, q):
    if t.exists:
        return (t.j + q) % 2
    return (t.j + 1 - q) % 2 if t.back(1).exists else t.j % 2


def out_pair(t):
    return t.j % 2 if t.exists else 1 - t.j % 2


def pool_splits_g2(t):
    return not t.exists and t.back(1).exists


def run_ticks(eng, tick):
    for j in range(TPI):
        tick(Tile(0, j))
    with eng.Fori(1, B) as image:
        for j in range(TPI):
            tick(Tile(image, j))
    for j in range(LAST_LAG):
        tick(Tile(B, j))


def conv_block_program(nc, x, xw3, xw1, vec, toep, raw_a, raw_b, out):
    f32 = mybir.dt.float32
    f32r = mybir.dt.float32r
    ALU = mybir.AluOpType
    ACT = mybir.ActivationFunctionType

    x_v = x.rearrange("b (k p) (j r) w -> b j p k (r w)", p=128, r=ROWS)
    out_v = out.rearrange("b (k p) (j r) w -> b j p k (r w)", p=128, r=ROWS)

    ctx = ExitStack()
    with ctx:
        def sb(name, shape, dt=f32):
            return ctx.enter_context(nc.sbuf_tensor(name, shape, dt))

        def sem(name):
            return ctx.enter_context(nc.semaphore(name))

        pi_hl = [sb(f"pi_{s}", [128, KC, C], f32r) for s in "hl"]
        post_hl = [sb(f"post_{s}", [128, KC, C], f32r) for s in "hl"]
        w1_hl = [sb(f"w1_{s}", [128, KC, E2], f32r) for s in "hl"]
        w2_hl = [sb(f"w2_{s}", [128, KE, C], f32r) for s in "hl"]
        toep_sb = sb("toep_sb", [GROUP * HW, 2 * GROUP * HW + W])
        toep3_sb = toep_sb[:, 0:2 * GROUP * HW].rearrange("p (e n) -> p e n", e=2)
        toep1_sb = toep_sb[0:W, 2 * GROUP * HW:]
        vecs = sb("vecs", [128, NVEC])
        bn = sb("bn", [128, 8, KC])
        b1 = sb("b1", [128, KE])
        b_out = sb("b_out", [128, KC])

        x_sb = sb("x_sb", [128, 2, KC, NPX])
        xw3_sb = sb("xw3_sb", [GROUP * HW, 2, GROUPS * 2, C])
        xw1_sb = sb("xw1_sb", [W, 2, C])
        xres_sb = sb("xres_sb", [128, 2, KC, NPX])
        res_h = sb("res_h", [128, RES_SLOTS, KC, NPX], f32r)
        res_l = sb("res_l", [128, RES_SLOTS, KC, NPX], f32r)
        t1_sb = sb("t1_sb", [128, T1_SLOTS, KC, T1_ROWS, T1_COLS])
        acc = sb("acc", [128, 2, KC, NPX])
        g1_h = sb("g1_h", [128, KC, NPX], f32r)
        g1_l = sb("g1_l", [128, KC, NPX], f32r)
        g2_sb = sb("g2_sb", [128, 2, NPX])
        g2_h = sb("g2_h", [128, KE, NPX], f32r)
        g2_l = sb("g2_l", [128, KE, NPX], f32r)
        area = [[ctx.enter_context(nc.psum_tensor(f"area_{p}{c}", [128, 2, 512], f32)) for c in range(2)]
                for p in range(2)]

        def raw_views(ap, sizes):
            views, at = [], 0
            for chunks, n in sizes:
                views.append(ap[:, at:at + chunks * n].rearrange("p (k n) -> p k n", k=chunks))
                at += chunks * n
            return views

        xres_flat = xres_sb[:, :, :, :].rearrange("p s k n -> p (s k n)")
        g2_flat = g2_sb[:, :, :].rearrange("p k n -> p (k n)")
        r_post, r_po, r_ffn2, r_fpw, r_p = raw_views(
            xres_flat, [(KC, C), (KC, C), (KC, E2), (KC, C), (KC, C)])
        r_pi, r_ffn1 = raw_views(g2_flat, [(KC, C), (KC, E2)])

        vecs_loaded, toep_loaded = sem("vecs_loaded"), sem("toep_loaded")
        pi_loaded, raw_a_loaded, raw_b_loaded = sem("pi_loaded"), sem("raw_a_loaded"), sem("raw_b_loaded")
        x_loaded = [sem(f"x_loaded{i}") for i in range(2)]
        xw_loaded = [sem(f"xw_loaded{i}") for i in range(2)]
        xres_loaded = [sem(f"xres_loaded{i}") for i in range(2)]
        out_stored = [sem(f"out_stored{i}") for i in range(2)]
        bn_step = sem("bn_step")
        root_done = sem("root_done")
        made = sem("made")
        w_copied = sem("w_copied")
        w_split = sem("w_split")
        pads_zeroed = sem("pads_zeroed")
        z_done = sem("z_done")
        resa_done = sem("resa_done")
        res2_done = sem("res2_done")
        res_h_done = sem("res_h_done")
        res_l_done = sem("res_l_done")
        t1_ready = sem("t1_ready")
        t1_taken = sem("t1_taken")
        conv_step = sem("conv_step")
        gelu1_done = sem("gelu1_done")
        g1_h_done = sem("g1_h_done")
        g1_l_done = sem("g1_l_done")
        f1_ready = sem("f1_ready")
        gelu2_done = sem("gelu2_done")
        g2_h_done = sem("g2_h_done")
        g2_l_done = sem("g2_l_done")
        out_ready = sem("out_ready")
        out_added = sem("out_added")

        def v(name, k):
            return vecs[:, VEC[name] + k:VEC[name] + k + 1]

        def vv(name):
            return vecs[:, VEC[name]:VEC[name] + KC]

        gain_x, shift_x, gain_z, centre_b = 4, 5, 6, 7

        def bn_col(row, k):
            return bn[:, row, k:k + 1]

        def tap_w(dh, dw, k):
            i = VEC["dw_w"] + 9 * k + 3 * (dh + 1) + (dw + 1)
            return vecs[:, i:i + 1]

        def banks(ap):
            return ap.rearrange("p (h n) -> p h n", h=2)

        def image_rows(ap):
            return ap.rearrange("p (r w) -> p r w", w=W)

        block = ctx.enter_context(nc.Block())

        @block.sync
        def _(sp):
            def load_xres(r):
                sp.dma_start(xres_sb[:, r.j % 2, :, :], x_v[r.image, r.j]).then_inc(xres_loaded[r.j % 2], 16)

            sp.dma_start(vecs[:, :], vec).then_inc(vecs_loaded, 16)
            sp.dma_start(toep_sb[:, :], toep).then_inc(toep_loaded, 16)

            def tick(t):
                if t.exists:
                    wait_for(sp, z_done, t.back(2), 2, 2)
                    sp.dma_start(xw3_sb[:, t.j % 2, :, :], xw3[t.image, t.j]).then_inc(xw_loaded[t.j % 2], 16)
                    sp.dma_start(xw1_sb[:, t.j % 2, :], xw1[t.image, t.j]).then_inc(xw_loaded[t.j % 2], 16)
                    wait_for(sp, res_l_done, t.back(2), 1, 1)
                    sp.dma_start(x_sb[:, t.j % 2, :, :], x_v[t.image, t.j]).then_inc(x_loaded[t.j % 2], 16)
                o = t.back(LAST_LAG)
                if o.exists:
                    wait_for(sp, out_added, o, 2, 2)
                    sp.dma_start(out_v[o.image, o.j], xres_sb[:, o.j % 2, :, :]).then_inc(out_stored[o.j % 2], 16)
                r = t.back(LAST_LAG - 2)
                if t.is_number(3):
                    sp.wait_ge(made, 3)
                    load_xres(r.back(1))
                if r.exists and not r.is_number(0):
                    wait_slot(sp, out_stored[r.j % 2], r, 2, 0)
                    load_xres(r)

            run_ticks(sp, tick)
            for s in range(2):
                sp.wait_ge(out_stored[s], 16 * TILES // 2)

        @block.tensor
        def _(pe):
            mm = nc.tensor.matmul

            def products(pairs, dst, stat, mov):
                n = len(pairs)
                for i, (ws, ms) in enumerate(pairs):
                    for p, (a, b) in enumerate(PASSES):
                        last = mm(dst, ws(stat[a]), ms(mov[b]), start=(i == 0 and p == 0),
                                  stop=(i == n - 1 and p == 2))
                return last

            def weight_products():
                pe.wait_ge(vecs_loaded, 16)
                pe.wait_ge(raw_a_loaded, 16)
                pe.wait_ge(raw_b_loaded, 16)
                pe.wait_ge(t1_taken, 16)
                for k in range(KC):
                    for q in range(KC):
                        last = mm(area[0][0][:, 0, k * C:(k + 1) * C], r_po[:, q, k * 128:(k + 1) * 128],
                                  r_post[:, q, :], start=(q == 0), stop=(q == KC - 1))
                last.then_inc(made, 1)
                for o in range(KE):
                    for q in range(KC):
                        mm(area[0][0][:, 1, 2 * o:2 * o + 1], r_ffn1[:, q, o * 128:(o + 1) * 128],
                           v("fpw_b", q), start=(q == 0), stop=(q == KC - 1))
                for k in range(KC):
                    for q in range(KC):
                        last = mm(area[0][1][:, k, 0:E2], r_fpw[:, q, k * 128:(k + 1) * 128], r_ffn1[:, q, :],
                                  start=(q == 0), stop=(q == KC - 1))
                last.then_inc(made, 1)
                pe.wait_ge(w_copied, 1)
                pe.wait_ge(res2_done, 12)
                for o in range(KC):
                    for i, (w, b) in enumerate(((r_p, "ffn2_b"), (r_post, "po_b"))):
                        for q in range(KC):
                            mm(area[1][0][:, 1, 2 * o:2 * o + 1], w[:, q, o * 128:(o + 1) * 128], v(b, q),
                               start=(i == 0 and q == 0), stop=(i == 1 and q == KC - 1))
                for k in range(KE):
                    for q in range(KC):
                        last = mm(area[1][1][:, k // 2, (k % 2) * C:(k % 2 + 1) * C],
                                  r_ffn2[:, q, k * 128:(k + 1) * 128], r_p[:, q, :],
                                  start=(q == 0), stop=(q == KC - 1))
                last.then_inc(made, 1)

            def t1_stage(s, t):
                if s.exists:
                    if s.is_number(0):
                        pe.wait_ge(w_split, 2)
                    if s.is_number(2):
                        pe.wait_ge(w_copied, 3)
                        pe.wait_ge(w_split, 8)
                    wait_for(pe, res_h_done, s, 1, 1)
                    wait_for(pe, res_l_done, s, 1, 1)
                    for c in range(KC):
                        wait_for(pe, gelu2_done, t.back(4), 4, 3 + c)
                        for h in range(2):
                            pairs = [(lambda w, k=k: w[:, k, c * 128:(c + 1) * 128],
                                      lambda m, k=k: m[:, s.j % RES_SLOTS, k, h * NHALF:(h + 1) * NHALF])
                                     for k in range(KC)]
                            last = products(pairs, area[t1_pair(t)][c][:, h, 0:NHALF], pi_hl, (res_h, res_l))
                        last.then_inc(t1_ready, 1)

            def z_stage(t):
                if t.exists:
                    if t.is_number(0):
                        pe.wait_ge(toep_loaded, 16)
                    if t.is_number(3):
                        pe.wait_ge(w_split, 6)
                    if t.back(4).exists:
                        wait_for(pe, out_added, t.back(4), 2, 2)
                    else:
                        wait_for(pe, t1_taken, t.back(2), 8, 8)
                    wait_slot(pe, xw_loaded[t.j % 2], t, 2, 1, 32)
                    for c in range(KC):
                        z = area[z_pair(t)][c][:, :, :].rearrange("p h n -> p (h n)")
                        for g in range(GROUPS):
                            for e in range(2):
                                rows = z[:, g * GROUP * Z_ROW:(g + 1) * GROUP * Z_ROW]
                                mm(rows.rearrange("p (r n) -> p r n", n=Z_ROW)[:, :, e * HW:(e + 1) * HW],
                                   xw3_sb[:, t.j % 2, 2 * g + e, c * 128:(c + 1) * 128], toep3_sb[:, e, :],
                                   start=True, stop=True)
                        mm(z[:, (ROWS - 1) * Z_ROW:(ROWS - 1) * Z_ROW + W],
                           xw1_sb[:, t.j % 2, c * 128:(c + 1) * 128], toep1_sb,
                           start=True, stop=True).then_inc(z_done, 1)

            def w1_stage(t, s, u):
                wait_for(pe, g1_h_done, u, 1, 1)
                wait_for(pe, g1_l_done, u, 1, 1)
                for c in range(KE):
                    dst = area[w1_pair(t, c // 2)][c % 2]
                    if t.exists:
                        if c < 2:
                            wait_for(pe, t1_taken, s, 8, 7 + c)
                        else:
                            wait_for(pe, res2_done, t, 4, 2 * (c - 1))
                    elif c < 2:
                        wait_for(pe, out_added, t.back(4), 2, 1 + c)
                    elif s.exists:
                        wait_for(pe, t1_taken, s, 8, 5 + c)
                    else:
                        wait_for(pe, gelu2_done, u, 4, c - 1)
                    for h in range(2):
                        pairs = [(lambda w, k=k: w[:, k, c * 128:(c + 1) * 128],
                                  lambda m, k=k: m[:, k, h * NHALF:(h + 1) * NHALF]) for k in range(KC)]
                        last = products(pairs, dst[:, h, 0:NHALF], w1_hl, (g1_h, g1_l))
                    last.then_inc(f1_ready, 1)

            def post_stage(t, u, last_ticks):
                for c in range(KC):
                    if last_ticks:
                        wait_for(pe, gelu2_done, t.back(4), 4, 3 + c)
                    else:
                        wait_for(pe, gelu2_done, u, 4, 1 + c)
                    if u.is_number(0):
                        pe.wait_ge(w_split, 8)
                    for h in range(2):
                        for k in range(KC):
                            for p, (a, b) in enumerate(PASSES):
                                mm(area[out_pair(t)][c][:, h, 0:NHALF], post_hl[a][:, k, c * 128:(c + 1) * 128],
                                   (res_h, res_l)[b][:, u.j % RES_SLOTS, k, h * NHALF:(h + 1) * NHALF],
                                   start=(k == 0 and p == 0), stop=False)

            def w2_stage(t, u):
                for q in range(KE // 2):
                    wait_for(pe, g2_h_done, u, 2, 1 + q)
                    wait_for(pe, g2_l_done, u, 2, 1 + q)
                    for c in range(KC):
                        for h in range(2):
                            for k in (2 * q, 2 * q + 1):
                                for p, (a, b) in enumerate(PASSES):
                                    last = mm(area[out_pair(t)][c][:, h, 0:NHALF],
                                              w2_hl[a][:, k, c * 128:(c + 1) * 128],
                                              (g2_h, g2_l)[b][:, k, h * NHALF:(h + 1) * NHALF],
                                              start=False, stop=(k == KE - 1 and p == 2))
                        if q == KE // 2 - 1:
                            last.then_inc(out_ready, 1)

            def tick(t):
                s, u = t.back(1), t.back(3)
                if t.is_number(1):
                    z_stage(t)
                    t1_stage(s, t)
                else:
                    t1_stage(s, t)
                    z_stage(t)
                if t.is_number(2):
                    weight_products()
                if u.exists:
                    last_ticks = not s.exists
                    if last_ticks:
                        post_stage(t, u, last_ticks)
                    w1_stage(t, s, u)
                    if not last_ticks:
                        post_stage(t, u, last_ticks)
                    w2_stage(t, u)

            run_ticks(pe, tick)

        @block.scalar
        def _(act):
            activation = nc.scalar.activation

            n_pi = KC * C
            act.wait_ge(bn_step, 1)
            activation(bn[:, 1, :], bn[:, 0, :], ACT.Sqrt).then_inc(root_done, 1)
            act.dma_start(g2_flat[:, 0:n_pi], raw_b[:, 0:n_pi]).then_inc(pi_loaded, 16)

            def copy_weights():
                act.wait_ge(made, 1)
                activation(r_p, area[0][0][:, 0, :].rearrange("p (k n) -> p k n", k=KC),
                           ACT.Copy).then_inc(w_copied, 1)
                act.wait_ge(made, 2)
                activation(w1_hl[0][:, :, :], area[0][1][:, :, :], ACT.Copy).then_inc(w_copied, 1)
                act.wait_ge(made, 3)
                activation(w2_hl[0][:, :, :].rearrange("p (a b) n -> p a (b n)", a=2), area[1][1][:, :, :],
                           ACT.Copy).then_inc(w_copied, 1)

            def res_h_stage(t):
                if t.exists:
                    wait_for(act, res2_done, t, 4, 4)
                    wait_for(act, out_ready, t.back(RES_SLOTS), 2, 2)
                    activation(res_h[:, t.j % RES_SLOTS], x_sb[:, t.j % 2, :, :],
                               ACT.Copy).then_inc(res_h_done, 1)

            def tick(t):
                if t.exists:
                    if t.is_number(0):
                        act.wait_ge(bn_step, BN_STEPS)
                    wait_slot(act, x_loaded[t.j % 2], t, 2, 1)
                    for k in range(KC):
                        a = x_sb[:, t.j % 2, k, :]
                        activation(a, a, ACT.Identity, bias=bn_col(shift_x, k),
                                   scale=bn_col(gain_x, k)).then_inc(resa_done, 1)
                    if t.is_number(0):
                        act.dma_start(xres_flat[:, 0:raw_a.shape[1]], raw_a).then_inc(raw_a_loaded, 16)
                        act.dma_start(g2_flat[:, n_pi:raw_b.shape[1]], raw_b[:, n_pi:]).then_inc(raw_b_loaded, 16)
                u = t.back(3)
                if u.exists:
                    for k in range(KC):
                        wait_for(act, conv_step, u, CONV_STEPS, CONV_STEPS - KC + 1 + k)
                        g = acc[:, u.j % 2, k, :]
                        activation(g, g, ACT.Gelu).then_inc(gelu1_done, 1)
                    wait_for(act, gelu1_done, u, 2, 2)
                    wait_for(act, f1_ready, u.back(1), 4, 4)
                    activation(g1_h[:, :, :], acc[:, u.j % 2, :, :], ACT.Copy).then_inc(g1_h_done, 1)
                s = t.back(1)
                if t.is_number(1):
                    res_h_stage(t)
                if s.exists:
                    here, before, after = (t1_sb[:, (s.j + d) % T1_SLOTS] for d in (0, -1, 1))
                    for k in range(KC):
                        wait_for(act, t1_ready, s, 2, 1 + k)
                        activation(here[:, k, 1:1 + ROWS, 1:1 + W].rearrange("p (h r) w -> p h r w", h=2),
                                   area[t1_pair(t)][k][:, :, 0:NHALF].rearrange("p h (r w) -> p h r w", w=W),
                                   ACT.Identity, bias=v("pi_b", k)).then_inc(t1_taken, 1)
                    for k in range(KC):
                        activation(before[:, k, T1_ROWS - 1, 1:1 + W], area[t1_pair(t)][k][:, 0, 0:W],
                                   ACT.Identity, bias=v("pi_b", k)).then_inc(t1_taken, 1)
                        activation(after[:, k, 0, 1:1 + W], area[t1_pair(t)][k][:, 1, NHALF - W:NHALF],
                                   ACT.Identity, bias=v("pi_b", k)).then_inc(t1_taken, 1)
                    wait_for(act, g1_l_done, s.back(2), 1, 1)
                    for k in range(KC):
                        activation(banks(acc[:, s.j % 2, k, :]), area[t1_pair(t)][k][:, :, 0:NHALF], ACT.Identity,
                                   bias=bn_col(centre_b, k), scale=tap_w(0, 0, k)).then_inc(t1_taken, 1)
                if not t.is_number(1):
                    res_h_stage(t)
                if t.is_number(2):
                    copy_weights()
                if u.is_number(0):
                    act.wait_ge(w_split, 6)
                if u.exists:
                    for q in range(KE // 2):
                        wait_for(act, g2_l_done, u, 2, q)
                        for i in range(2):
                            c = 2 * q + i
                            wait_for(act, f1_ready, u, 4, 1 + c)
                            activation(banks(g2_sb[:, i, :]), area[w1_pair(t, q)][i][:, :, 0:NHALF], ACT.Gelu,
                                       bias=b1[:, c:c + 1]).then_inc(gelu2_done, 1)
                        wait_for(act, gelu2_done, u, 4, 2 + 2 * q)
                        if q == 0:
                            wait_for(act, out_ready, u.back(1), 2, 2)
                        activation(g2_h[:, 2 * q:2 * q + 2, :], g2_sb[:, :, :], ACT.Copy).then_inc(g2_h_done, 1)

            run_ticks(act, tick)

        def bn_program(dve):
            n = 0
            tt, ts, stt = nc.vector.tensor_tensor, nc.vector.tensor_scalar, nc.vector.scalar_tensor_tensor

            def step(ins):
                nonlocal n
                n += 1
                ins.then_inc(bn_step, 1)
                dve.wait_ge(bn_step, n)

            var, y, tmp, s = (bn[:, i, :] for i in (0, 1, 2, 3))
            step(ts(var, vv("var"), EPS, None, ALU.add))
            dve.wait_ge(root_done, 1)
            step(nc.vector.reciprocal(y, y))
            for _ in range(2):
                step(tt(tmp, y, y, ALU.mult))
                step(tt(tmp, tmp, var, ALU.mult))
                step(ts(tmp, tmp, -0.5, 1.5, ALU.mult, ALU.add))
                step(tt(y, y, tmp, ALU.mult))
            step(tt(s, vv("gamma"), y, ALU.mult))
            step(tt(bn[:, gain_x, :], vv("ar"), s, ALU.mult))
            step(tt(bn[:, gain_z, :], vv("ai"), s, ALU.mult))
            step(tt(tmp, vv("mean"), s, ALU.mult))
            step(tt(tmp, vv("beta"), tmp, ALU.subtract))
            step(tt(bn[:, shift_x, :], vv("ar"), tmp, ALU.mult))
            for k in range(KC):
                step(stt(bn_col(centre_b, k), v("pi_b", k), tap_w(0, 0, k), v("dw_b", k), ALU.mult, ALU.add))
            return n

        @block.vector
        def _(dve):
            tt, stt, copy = nc.vector.tensor_tensor, nc.vector.scalar_tensor_tensor, nc.vector.tensor_copy

            dve.wait_ge(vecs_loaded, 16)
            assert bn_program(dve) == BN_STEPS

            def split_weight(hl, raw, loaded, steps):
                dve.wait_ge(loaded, 16)
                copy(hl[0][:, :, :], raw).then_inc(w_split, 1)
                dve.wait_ge(w_split, steps + 1)
                tt(hl[1][:, :, :], raw, hl[0][:, :, :].bitcast(f32), ALU.subtract).then_inc(w_split, 1)

            dve.wait_ge(pads_zeroed, 1)

            def split_products(wn_hl, count):
                dve.wait_ge(made, count)
                dve.wait_ge(w_copied, count)
                w = [i[:, :, :].rearrange("p k n -> p (k n)").rearrange("p (a b) -> p a b", a=2) for i in wn_hl]
                pair = area[count - 2]
                tt(w[1], pair[1][:, :, :], w[0].bitcast(f32), ALU.subtract).then_inc(w_split, 1)
                bias, n, first = (b1, KE, VEC["ffn1_b"]) if count == 2 else (b_out, KC, VEC["post_b"])
                tt(bias[:, :], pair[0][:, 1, 0:2 * n].rearrange("p (o two) -> p o two", two=2)[:, :, 0],
                   vecs[:, first:first + n], ALU.add).then_inc(w_split, 1)

            def tick(t):
                o = t.back(4)

                def add_out():
                    if not o.exists:
                        return
                    wait_slot(dve, xres_loaded[o.j % 2], o, 2, 1)
                    for k in range(KC):
                        wait_for(dve, out_ready, o, 2, 1 + k)
                        y = banks(xres_sb[:, o.j % 2, k, :])
                        stt(y, area[out_pair(t.back(1))][k][:, :, 0:NHALF], b_out[:, k:k + 1], y,
                            ALU.add, ALU.add).then_inc(out_added, 1)
                u = t.back(3)

                def split_g1():
                    if not u.exists:
                        return
                    wait_for(dve, g1_h_done, u, 1, 1)
                    tt(g1_l[:, :, :], acc[:, u.j % 2, :, :], g1_h[:, :, :].bitcast(f32),
                       ALU.subtract).then_inc(g1_l_done, 1)
                s, w = t.back(1), t.back(2)

                def taps(first, last):
                    if not w.exists:
                        return
                    for i in range(first, last):
                        dh, dw = TAPS[i]
                        lo = 1 if w.j == 0 and dh == -1 else 0
                        hi = ROWS - 1 if w.j == TPI - 1 and dh == 1 else ROWS
                        if i == 0:
                            wait_for(dve, t1_taken, w, 8, 8)
                        if dh == 1 and w.j != TPI - 1:
                            wait_for(dve, t1_taken, w.back(-1), 8, 6)
                        for k in range(KC):
                            if i > 0:
                                wait_for(dve, conv_step, w, CONV_STEPS, KC * (i - 1) + k + 1)
                            src = t1_sb[:, w.j % T1_SLOTS, k, 1 + lo + dh:1 + hi + dh, 1 + dw:1 + dw + W]
                            a = image_rows(acc[:, w.j % 2, k, :])[:, lo:hi, :]
                            stt(a, src, tap_w(dh, dw, k), a, ALU.mult, ALU.add).then_inc(conv_step, 1)

                def split_g2(q):
                    if not u.exists or pool_splits_g2(t):
                        return
                    wait_for(dve, g2_h_done, u, 2, 1 + q)
                    tt(g2_l[:, 2 * q:2 * q + 2, :], g2_sb[:, :, :], g2_h[:, 2 * q:2 * q + 2, :].bitcast(f32),
                       ALU.subtract).then_inc(g2_l_done, 1)

                if s.exists:
                    add_out()
                    split_g1()
                    taps(0, 2)
                else:
                    taps(0, 2)
                    split_g1()
                    add_out()
                if t.exists:
                    wait_for(dve, resa_done, t, 2, 2)
                    for k in range(KC):
                        wait_for(dve, z_done, t, 2, 1 + k)
                        z = area[z_pair(t)][k][:, :, :].rearrange("p h n -> p (h n)")[:, 0:ROWS * Z_ROW]
                        z = z.rearrange("p (r n) -> p r n", n=Z_ROW)
                        for e in range(2):
                            y = image_rows(x_sb[:, t.j % 2, k, :])[:, :, 1 - e:W:2]
                            stt(y, z[:, :, e * HW:(e + 1) * HW], bn_col(gain_z, k), y,
                                ALU.mult, ALU.add).then_inc(res2_done, 1)
                if t.is_number(0):
                    split_weight(pi_hl, r_pi, pi_loaded, 0)
                    wait_for(dve, res_h_done, t, 1, 1)
                    tt(res_l[:, 0], x_sb[:, 0, :, :], res_h[:, 0].bitcast(f32),
                       ALU.subtract).then_inc(res_l_done, 1)
                if s.exists:
                    taps(2, 5)
                    split_g2(0)
                    taps(5, 6)
                    split_g2(1)
                    taps(6, 7)
                    if t.is_number(2):
                        split_products(w1_hl, 2)
                    taps(7, 8)
                else:
                    taps(2, 8)
                    split_g2(0)
                    split_g2(1)
                if t.is_number(2):
                    split_products(w2_hl, 3)
                if t.is_number(1):
                    split_weight(post_hl, r_post, raw_a_loaded, 2)

            run_ticks(dve, tick)

        @block.gpsimd
        def _(pool):
            t1_all = t1_sb[:, :, :, :, :].rearrange("p s k r w -> p (s k r) w")
            nc.gpsimd.memset(t1_all[:, :, 0:T1_COLS:T1_COLS - 1], 0.0).then_inc(pads_zeroed, 1)

            def tick(t):
                if t.exists and not t.is_number(0):
                    wait_for(pool, res_h_done, t, 1, 1)
                    nc.gpsimd.tensor_tensor(res_l[:, t.j % RES_SLOTS], x_sb[:, t.j % 2, :, :],
                                            res_h[:, t.j % RES_SLOTS].bitcast(f32),
                                            ALU.subtract).then_inc(res_l_done, 1)
                u = t.back(3)
                if pool_splits_g2(t):
                    for q in range(KE // 2):
                        wait_for(pool, g2_h_done, u, 2, 1 + q)
                        nc.gpsimd.tensor_tensor(g2_l[:, 2 * q:2 * q + 2, :], g2_sb[:, :, :],
                                                g2_h[:, 2 * q:2 * q + 2, :].bitcast(f32),
                                                ALU.subtract).then_inc(g2_l_done, 1)

            run_ticks(pool, tick)


def kernel(**inputs):
    import numpy as _np
    import concourse.bacc as _bacc
    from concourse import mybir as _mybir
    from concourse.bass_utils import run_bass_kernel_spmd as _run

    a = {k.replace("L0_conv_", ""): _np.asarray(i) for k, i in inputs.items()}

    def by_partition(vector):
        return vector.reshape(-1, 128).T

    def by_rows(matrix):
        return matrix.reshape(-1, 128, matrix.shape[1]).transpose(1, 0, 2).reshape(128, -1)

    vec = _np.concatenate(
        [by_partition(a[n]) for n in ("bn_gamma", "bn_beta", "bn_mean", "bn_var")]
        + [by_partition(a["alpha_real"].reshape(-1)), by_partition(a["alpha_imag"].reshape(-1))]
        + [by_partition(a[n]) for n in ("pi_b", "dw_b", "fpw_b", "ffn2_b", "po_b", "post_b", "ffn1_b")]
        + [a["dw_w"].reshape(KC, 128, 9).transpose(1, 0, 2).reshape(128, KC * 9)], axis=1)
    d = _np.arange(W)[None, :] - _np.arange(W)[:, None]
    odd = d % 2 != 0
    toep = _np.where(odd, -(2.0 / W) / _np.tan(_np.pi * _np.where(odd, d, 1) / W), 0.0).astype(_np.float32)
    toep1 = _np.concatenate([toep[:, 1::2], toep[:, 0::2]], axis=1)
    toep3 = _np.zeros((GROUP, HW, 2, GROUP, HW), _np.float32)
    for r in range(GROUP):
        for e in range(2):
            toep3[r, :, e, r, :] = toep[e::2, 1 - e::2]
    rows = a["x"].reshape(B, C, TPI, ROWS, HW, 2)
    xw3 = rows[:, :, :, :ROWS - 1].reshape(B, C, TPI, GROUPS, GROUP, HW, 2).transpose(0, 2, 4, 5, 3, 6, 1)
    xw1 = rows[:, :, :, ROWS - 1].transpose(0, 2, 3, 4, 1)

    arrays = {
        "x": a["x"], "xw3": xw3.reshape(B, TPI, GROUP * HW, GROUPS * 2, C), "xw1": xw1.reshape(B, TPI, W, C), "vec": vec,
        "toep": _np.concatenate([toep3.reshape(GROUP * HW, 2 * GROUP * HW),
                                 _np.pad(toep1, ((0, GROUP * HW - W), (0, 0)))], axis=1),
        "raw_a": _np.concatenate([by_rows(a["post_w"].T), by_rows(a["po_w"]), by_rows(a["ffn2_w"]),
                                  by_rows(a["fpw_w"])], axis=1),
        "raw_b": _np.concatenate([by_rows(a["pi_w"].T), by_rows(a["ffn1_w"].T)], axis=1),
    }
    arrays = {k: _np.ascontiguousarray(i) for k, i in arrays.items()}
    nc = _bacc.Bacc("TRN2", target_bir_lowering=False, num_devices=1)
    args = [nc.dram_tensor(f"in_{k}", i.shape, _mybir.dt.from_np(i.dtype), kind="ExternalInput").ap()
            for k, i in arrays.items()]
    out = nc.dram_tensor("out_0", (B, C, H, W), _mybir.dt.float32, kind="ExternalOutput").ap()
    conv_block_program(nc, *args, out)
    r = _run(nc, [{f"in_{k}": i for k, i in arrays.items()}], core_ids=[0])
    return r.results[0]["out_0"]
```
